# Optimizing a Trainium2 kernel written in Bass

```python
import numpy as np
import jax
import jax.numpy as jnp

def _softmax(x, axis=-1):
    return jax.nn.softmax(x, axis=axis)

def _gelu(x):
    return jax.nn.gelu(x, approximate=True)

def _silu(x):
    return jax.nn.silu(x)

def _sigmoid(x):
    return jax.nn.sigmoid(x)

def _layernorm(x, axis=-1, eps=1e-05):
    m = jnp.mean(x, axis=axis, keepdims=True)
    v = jnp.var(x, axis=axis, keepdims=True)
    return (x - m) / jnp.sqrt(v + eps)

def _scatter_add(tgt, idx, src, axis=0):
    return tgt.at[idx].add(src)

def _segment_sum(src, seg, n):
    return jax.ops.segment_sum(src, seg, n)
kernel_name = 'mk_xattn_ffn_d1_seqx_r4_36979a'

def setup_inputs(seed: int=0):
    np.random.seed(seed)
    _w = jnp.asarray

    def _rec_inputs():
        import jax
        import jax.numpy as jnp
        _rk = jax.random.key(seed)
        x = -0.0003929 + 0.9999 * jax.random.normal(jax.random.fold_in(_rk, 1), (8, 256, 256), jnp.float32)
        _lenS = 256 - jax.random.randint(jax.random.fold_in(_rk, 7), (8,), 0, max(1, 256 // 4) + 1, jnp.int32)
        _lenS2 = 256 - jax.random.randint(jax.random.fold_in(_rk, 8), (8,), 0, max(1, 256 // 4) + 1, jnp.int32)
        _ctx_1024P = jax.random.normal(jax.random.fold_in(_rk, 11), (8, 16, 256), jnp.float32)
        _ctx_1024c = jax.random.dirichlet(jax.random.fold_in(_rk, 511), 0.3 * jnp.ones((16,), jnp.float32), (8, 256))
        _ctx_1024t = jnp.einsum('bsk,bkd->bsd', _ctx_1024c, _ctx_1024P)
        _ctx_1024t = _ctx_1024t * jax.lax.rsqrt(jnp.mean(jnp.square(_ctx_1024t)) + 1e-12) * 0.953939
        ctx_1024 = 2.81802e-05 + 1.00001 * (_ctx_1024t + 0.3 * jax.random.normal(jax.random.fold_in(_rk, 611), (8, 256, 256), jnp.float32))
        _validS = jnp.arange(256)[None, :] < _lenS[:, None]
        _validS2 = jnp.arange(256)[None, :] < _lenS2[:, None]
        _causal = jnp.tril(jnp.ones((256, 256), dtype=bool))
        mask_BxSxS2_ff1 = jnp.where(jnp.ones((8, 256, 256), dtype=bool), 1.0, 0.0).astype(jnp.float32)
        mask_BxS2_ff1 = jnp.where(jnp.ones((8, 256), dtype=bool), 1.0, 0.0).astype(jnp.float32)
        return (x, ctx_1024, mask_BxSxS2_ff1, mask_BxS2_ff1)
    x, ctx_1024, mask_BxSxS2_ff1, mask_BxS2_ff1 = _rec_inputs()

    def _L0_xattn_setup():
        import jax, jax.numpy as jnp
        import numpy as np
        key = jax.random.key(seed)
        ks = jax.random.split(key, 5)
        B, S, D = (8, 512, 256)
        return {'query': jax.random.normal(ks[0], (B, S, D), dtype=jnp.float32), 'key': jax.random.normal(ks[1], (B, S, D), dtype=jnp.float32), 'value': jax.random.normal(ks[2], (B, S, D), dtype=jnp.float32), 'cell_mask': jnp.ones((B, S, S), dtype=jnp.float32), 'seq_mask': jnp.ones((B, S), dtype=jnp.float32), 'W_k': jax.random.normal(ks[3], (D, D), dtype=jnp.float32) * (1.0 / np.sqrt(D)), 'b_k': jnp.zeros((D,), dtype=jnp.float32), 'W_o': jax.random.normal(ks[4], (D, D), dtype=jnp.float32) * (1.0 / np.sqrt(D)), 'b_o': jnp.zeros((D,), dtype=jnp.float32)}
    _L0_xattn_all = _L0_xattn_setup()
    _L0_xattn_in = {k: v for k, v in _L0_xattn_all.items() if k in ('W_k', 'b_k', 'W_o', 'b_o')}
    del _L0_xattn_all

    def _L0_ffn_setup():
        import jax, jax.numpy as jnp
        import numpy as np
        EPS = 1e-05
        LN_EPS = 1e-05
        NUM_EXPERTS = 8
        TOP_K = 2
        HIDDEN = 256
        INTER = 512

        def _swiglu(x, wg, wu, wd):
            return jax.nn.silu(x @ wg) * (x @ wu) @ wd
        key = jax.random.key(seed)
        ks = jax.random.split(key, 10)
        B, S, H, I, E = (8, 1024, HIDDEN, INTER, NUM_EXPERTS)
        std_h = 1.0 / np.sqrt(H)
        std_i = 1.0 / np.sqrt(I)
        return {'x': jax.random.normal(ks[0], (B, S, H), dtype=jnp.float32), 'ln_scale': jnp.ones((H,), dtype=jnp.float32), 'ln_bias': jnp.zeros((H,), dtype=jnp.float32), 'gate_w': jax.random.normal(ks[1], (E, H), dtype=jnp.float32) * 0.01, 'Wg': jax.random.normal(ks[2], (E, H, I), dtype=jnp.float32) * std_h, 'Wu': jax.random.normal(ks[3], (E, H, I), dtype=jnp.float32) * std_h, 'Wd': jax.random.normal(ks[4], (E, I, H), dtype=jnp.float32) * std_i, 'sWg': jax.random.normal(ks[5], (H, I), dtype=jnp.float32) * std_h, 'sWu': jax.random.normal(ks[6], (H, I), dtype=jnp.float32) * std_h, 'sWd': jax.random.normal(ks[7], (I, H), dtype=jnp.float32) * std_i}
    _L0_ffn_all = _L0_ffn_setup()
    _L0_ffn_in = {k: v for k, v in _L0_ffn_all.items() if k in ('ln_scale', 'ln_bias', 'gate_w', 'Wg', 'Wu', 'Wd', 'sWg', 'sWu', 'sWd')}
    del _L0_ffn_all
    return {'x': x, 'ctx_1024': ctx_1024, 'mask_BxSxS2_ff1': mask_BxSxS2_ff1, 'mask_BxS2_ff1': mask_BxS2_ff1, 'L0_xattn_W_k': _L0_xattn_in['W_k'], 'L0_xattn_b_k': _L0_xattn_in['b_k'], 'L0_xattn_W_o': _L0_xattn_in['W_o'], 'L0_xattn_b_o': _L0_xattn_in['b_o'], 'L0_ffn_ln_scale': _L0_ffn_in['ln_scale'], 'L0_ffn_ln_bias': _L0_ffn_in['ln_bias'], 'L0_ffn_gate_w': _L0_ffn_in['gate_w'], 'L0_ffn_Wg': _L0_ffn_in['Wg'], 'L0_ffn_Wu': _L0_ffn_in['Wu'], 'L0_ffn_Wd': _L0_ffn_in['Wd'], 'L0_ffn_sWg': _L0_ffn_in['sWg'], 'L0_ffn_sWu': _L0_ffn_in['sWu'], 'L0_ffn_sWd': _L0_ffn_in['sWd']}

def reference(x, ctx_1024, mask_BxSxS2_ff1, mask_BxS2_ff1, L0_xattn_W_k, L0_xattn_b_k, L0_xattn_W_o, L0_xattn_b_o, L0_ffn_ln_scale, L0_ffn_ln_bias, L0_ffn_gate_w, L0_ffn_Wg, L0_ffn_Wu, L0_ffn_Wd, L0_ffn_sWg, L0_ffn_sWu, L0_ffn_sWd):
    import jax
    import jax.numpy as jnp

    def _L0_xattn_ref(query, key, value, cell_mask, seq_mask, W_k, b_k, W_o, b_o):
        import jax, jax.numpy as jnp
        import numpy as np
        k_proj = jnp.einsum('bkd,qd->bkq', key, W_k) + b_k
        scores = jnp.einsum('bqd,bkd->bqk', query, k_proj)
        scores = scores + jnp.log(cell_mask) + jnp.log(seq_mask)[:, None, :]
        p_attn = jax.nn.softmax(scores, axis=-1)
        x = jnp.einsum('bqk,bkd->bqd', p_attn, value)
        return jnp.einsum('bqd,od->bqo', x, W_o) + b_o

    def _L0_ffn_ref(x, ln_scale, ln_bias, gate_w, Wg, Wu, Wd, sWg, sWu, sWd):
        import jax, jax.numpy as jnp
        import numpy as np
        EPS = 1e-05
        LN_EPS = 1e-05
        NUM_EXPERTS = 8
        TOP_K = 2
        HIDDEN = 256
        INTER = 512

        def _swiglu(x, wg, wu, wd):
            return jax.nn.silu(x @ wg) * (x @ wu) @ wd
        B, S, H = x.shape
        xf = x.reshape(-1, H)
        mu = jnp.mean(xf, axis=-1, keepdims=True)
        var = jnp.var(xf, axis=-1, keepdims=True)
        xn = (xf - mu) * jax.lax.rsqrt(var + LN_EPS) * ln_scale + ln_bias
        logits = xn @ gate_w.T
        probs = jax.nn.softmax(logits, axis=-1)
        tk_probs, tk_idx = jax.lax.top_k(probs, TOP_K)
        tk_probs = tk_probs / (jnp.sum(tk_probs, axis=-1, keepdims=True) + EPS)
        onehot = tk_idx[..., None] == jnp.arange(NUM_EXPERTS)[None, None, :]
        w = jnp.sum(tk_probs[..., None] * onehot.astype(tk_probs.dtype), axis=1)
        out = _swiglu(xf, sWg, sWu, sWd)
        for e in range(NUM_EXPERTS):
            out = out + w[:, e:e + 1] * _swiglu(xf, Wg[e], Wu[e], Wd[e])
        return out.reshape(B, S, H)
    x = x + _L0_xattn_ref(_layernorm(x, axis=-1), ctx_1024, ctx_1024, mask_BxSxS2_ff1, mask_BxS2_ff1, L0_xattn_W_k, L0_xattn_b_k, L0_xattn_W_o, L0_xattn_b_o)
    x = x + _L0_ffn_ref(_layernorm(x, axis=-1), L0_ffn_ln_scale, L0_ffn_ln_bias, L0_ffn_gate_w, L0_ffn_Wg, L0_ffn_Wu, L0_ffn_Wd, L0_ffn_sWg, L0_ffn_sWu, L0_ffn_sWd)
    return x

_drawn_inputs = setup_inputs


def setup_inputs(seed=0):
    import zlib

    import numpy as np

    out = dict(_drawn_inputs(seed))
    spreads = {'L0_xattn_b_k': (0.0, 0.1),
     'L0_xattn_b_o': (0.0, 0.1),
     'L0_ffn_ln_scale': (1.0, 0.2),
     'L0_ffn_ln_bias': (0.0, 0.1)}
    factors = {}
    for name, (base, spread) in spreads.items():
        noise = np.random.default_rng([zlib.crc32(name.encode()), seed]).standard_normal(out[name].shape)
        drawn = base * np.exp(spread * noise) if base else spread * noise
        out[name] = jnp.asarray(drawn.astype(out[name].dtype))
    for name, factor in factors.items():
        out[name] = (out[name] * factor).astype(out[name].dtype)
    return out
```

```python
from contextlib import ExitStack

import concourse.bass as bass
from concourse import mybir
from concourse.alu_op_type import AluOpType as ALU

ACT = mybir.ActivationFunctionType
AX = mybir.AxisListType
F32 = mybir.dt.float32
F16 = mybir.dt.float16
BF16 = mybir.dt.bfloat16
I32 = mybir.dt.int32
U32 = mybir.dt.uint32

P = 128
B, S, D = 8, 256, 256
QT = S // P
DC = D // P
T = B * QT
N = B * S
E, TOP_K = 8, 2
I = 512
IC = I // P
CH = D * I // P
ET = N * TOP_K // P + E - 1
ROW = D + 2
LN_EPS = 1e-5
EPS = 1e-5
TINY = 2.0 ** -64
MASKED = -1e30

SX, SW, SG, SH = 2.0 ** 8, 2.0 ** 6, 2.0 ** 8, 4.0

CHUNKS_A = 8
FIRST_CHUNKS = 3


def at_least(eng, sem, count):
    if not (isinstance(count, int) and count <= 0):
        eng.wait_ge(sem, count)


def alone(eng, passed):
    eng.sem_inc(passed, 1)


def xattn_moe_kernel(nc, x, ctx_kd, ctx_dk, cell_mask, seq_mask, wk_t, wo_t, b_o, cols, experts, dispatch, out):
    with ExitStack() as stack:
        def sb(name, shape, dt=F32):
            return stack.enter_context(nc.sbuf_tensor(name, shape, dt))

        def sem(name):
            return stack.enter_context(nc.semaphore(name))

        bank = [stack.enter_context(nc.psum_tensor(f"bank{i}", [P, 512], F32)) for i in range(8)]

        w_hi = sb("w_hi", [P, 3 * (E + 1) * CH], F16)
        w_lo = sb("w_lo", [P, 3 * (E + 1) * CH], F16)
        stage = [sb(f"stage{i}", [P, CH]) for i in range(2)]
        wk = sb("wk", [P, DC, D])
        wo = sb("wo", [P, DC, D])
        bo = sb("bo", [P, D])
        col = sb("col", [P, DC, 3 + E])
        gate_bias = sb("gate_bias", [P, DC, 2 * E])
        gate_s = sb("gate_s", [P, DC, E])
        gate_hi = sb("gate_hi", [P, DC, E], F16)
        gate_lo = sb("gate_lo", [P, DC, E], F16)
        ident = sb("ident", [P, P])
        ones_b = sb("ones_b", [P, P], BF16)
        before = sb("before", [P, P], BF16)
        desc = sb("desc", [P, E, T])
        tile_no = sb("tile_no", [1, ET, E], BF16)
        tiny = sb("tiny", [P, 1])

        x1 = sb("x1", [P, T, D])
        rows = sb("rows", [P, T, ROW])
        xt_hi = sb("xt_hi", [P, T, DC, P], F16)
        xt_lo = sb("xt_lo", [P, T, DC, P], F16)
        mv3 = sb("mv3", [P, T, 2])

        work = sb("work", [P, 15 * 512])
        slot = [work[:, i * 512:(i + 1) * 512] for i in range(15)]

        def two(ap):
            return ap.rearrange("p (t d) -> p t d", t=2)

        x_in = [two(slot[0]), two(slot[1])]
        c_kd = [two(slot[2]), two(slot[3])]
        c_dk = [two(slot[4]), two(slot[5])]
        cm = [two(slot[6]), two(slot[7])]
        xln, x_t, k_t, p, p_t, a_t, xf = [two(slot[i]) for i in range(8, 15)]
        log_m = sb("log_m", [P, QT, S])
        sm = sb("sm", [P, S])
        sm_log = sb("sm_log", [P, S])

        ones = slot[13][:, 0:P]
        pad_row = rows[:, T - 1, :]

        stats = sb("stats", [P, 4, 6])
        stats3 = sb("stats3", [P, 2, 6])
        mv_xf = sb("mv_xf", [P, QT, 2])
        mv = sb("mv", [P, 4, 2])
        ve = sb("ve", [P, 4])
        r0 = sb("r0", [P, 4])
        r2 = sb("r2", [P, 4])
        rstd = sb("rstd", [P, 4])
        nmax = sb("nmax", [P, QT])
        sums = [sb(f"sums{i}", [P, QT]) for i in range(2)]
        rinv = sb("rinv", [P, QT])

        xg = [slot[i][:, 0:ROW] for i in range(4)]
        g_act = slot[4]
        h = slot[5]
        h_hi = slot[6].bitcast(F16)[:, 0:I]
        h_lo = slot[6].bitcast(F16)[:, I:2 * I]
        xe_hi = [slot[7].bitcast(F16)[:, i * D:(i + 1) * D].rearrange("p (c t) -> p c t", c=DC) for i in range(2)]
        xe_lo = [slot[7].bitcast(F16)[:, (2 + i) * D:(3 + i) * D].rearrange("p (c t) -> p c t", c=DC) for i in range(2)]
        y = [slot[8 + i // 2][:, (i % 2) * D:(i % 2 + 1) * D] for i in range(4)]
        tok = sb("tok", [P, 4], U32)

        def et(i):
            return slot[10 + i // 4][:, (i % 4) * P:(i % 4 + 1) * P].rearrange("p (e t) -> p e t", e=E)

        def by_tile(ap):
            return ap.rearrange("p e t -> p t e")

        logit, eq, one1, one2, tmp, expo, cols_incl, offs, zero_first = [et(i) for i in range(9)]
        both = sb("both", [P, E, T], BF16)
        small = sb("small", [P, 12, T])
        ve3, r03, r23, rs3, nm3, m1, mx, m2, z, e2, w1, w2 = [small[:, i, :] for i in range(12)]
        sg_c = sb("sg_c", [P, 2, E])
        n_e = sb("n_e", [P, 4, E])
        n_int = sb("n_int", [P, 2, E], I32)
        posf = sb("posf", [P, T])
        pos = [sb(f"pos{i}", [P, T], U32) for i in range(2)]
        te_cmp = slot[13][0:1, 0:ET * E].rearrange("p (i e) -> p i e", e=E)
        te_f = slot[13][0:1, 320:320 + 2 * ET].rearrange("p (a i) -> p a i", a=2)
        te = sb("te", [1, ET], I32)

        consts_in = sem("consts_in")
        x_loaded = [sem(f"x_loaded{i}") for i in range(2)]
        kd_loaded = [sem(f"kd_loaded{i}") for i in range(2)]
        dk_loaded = [sem(f"dk_loaded{i}") for i in range(2)]
        cm_loaded = [sem(f"cm_loaded{i}") for i in range(2)]
        sm_loaded = sem("sm_loaded")
        w_loaded = [sem(f"w_loaded{i}") for i in range(2)]
        xg_loaded = [sem(f"xg_loaded{i}") for i in range(4)]
        pads_written = sem("pads_written")
        rows_sent = [sem(f"rows_sent{i}") for i in range(2)]
        shared_stored = [sem(f"shared_stored{i}") for i in range(2)]
        added = sem("added")
        consts_made = sem("consts_made")
        tri_zero = sem("tri_zero")
        gates_made = sem("gates_made")
        gb_summed, gb_copied = sem("gb_summed"), sem("gb_copied")
        xln_ready, tx_done, xt_ready = sem("xln_ready"), sem("tx_done"), sem("xt_ready")
        k_done, kt_ready, s_done = sem("k_done"), sem("kt_ready"), sem("s_done")
        xb_ready, logm_made, seqm_ready, pen_ready, logm_ready = (
            sem("xb_ready"), sem("logm_made"), sem("seqm_ready"), sem("pen_ready"), sem("logm_ready"))
        pen_added, smp_ready = sem("pen_added"), sem("smp_ready")
        s_masked, max_ready, p_ready = sem("s_masked"), sem("max_ready"), sem("p_ready")
        tp_done, pt_ready, a_done, at_ready, o_done = (
            sem("tp_done"), sem("pt_ready"), sem("a_done"), sem("at_ready"), sem("o_done"))
        rinv_ready, x1_ready = sem("rinv_ready"), sem("x1_ready")
        stats_ready, mv_ready, ve_ready, ln_ready, r0_ready, nt_ready = (
            sem("stats_ready"), sem("mv_ready"), sem("ve_ready"), sem("ln_ready"), sem("r0_ready"), sem("nt_ready"))
        dve_passed, pool_passed = sem("dve_passed"), sem("pool_passed")
        row_ready, mvx_ready = sem("row_ready"), sem("mvx_ready")
        xf_ready, st3_ready, mv3_ready, txf_done, xhi_ready, xlo_ready, lg_done = (
            sem("xf_ready"), sem("st3_ready"), sem("mv3_ready"), sem("txf_done"), sem("xhi_ready"),
            sem("xlo_ready"), sem("lg_done"))
        whi_ready, wlo_ready = sem("whi_ready"), sem("wlo_ready")
        route = sem("route")
        d_ready, expo_ready, ve3_ready, r03_ready, both_ready, cum_done, pos_ready = (
            sem("d_ready"), sem("expo_ready"), sem("ve3_ready"), sem("r03_ready"), sem("both_ready"),
            sem("cum_done"), sem("pos_ready"))
        w_ready = sem("w_ready")
        g_done, u_done, act_ready, h_ready, th_done, hhi_ready, hlo_ready, d_done, y_ready = (
            sem("g_done"), sem("u_done"), sem("act_ready"), sem("h_ready"), sem("th_done"), sem("hhi_ready"),
            sem("hlo_ready"), sem("d_done"), sem("y_ready"))
        tg_done, ghi_ready, glo_ready = sem("tg_done"), sem("ghi_ready"), sem("glo_ready")

        x_v = x.rearrange("(b t p) d -> b p t d", t=QT, p=P)
        kd_v = ctx_kd.rearrange("b (t p) d -> b p t d", p=P)
        dk_v = ctx_dk.rearrange("b (c p) k -> b p c k", p=P)
        cm_v = cell_mask.rearrange("b (t p) k -> b p t k", p=P)
        disp_v = dispatch.rearrange("(i p) r -> i p r", p=P)
        out_v = out.rearrange("(t p) d -> t p d", p=P)

        def ix(ap, i):
            return ap[bass.ds(i, 1)].rearrange("o p t d -> (o p) t d") if len(ap.shape) == 4 else \
                ap[bass.ds(i, 1)].rearrange("o p d -> (o p) d")

        block = stack.enter_context(nc.Block())

        @block.sync
        def _(sp):
            def load_x(b, q):
                at_least(sp, xln_ready, b - 1)
                at_least(sp, xb_ready, b - 1)
                sp.dma_start(x_in[q], ix(x_v, b)).then_inc(x_loaded[q], 16)

            def load_ctx(b, q):
                at_least(sp, k_done, b - 1)
                sp.dma_start(c_dk[q], ix(dk_v, b)).then_inc(dk_loaded[q], 16)
                at_least(sp, a_done, b - 1)
                sp.dma_start(c_kd[q], ix(kd_v, b)).then_inc(kd_loaded[q], 16)

            def load_mask(b, q):
                at_least(sp, logm_ready, b - 1)
                sp.dma_start(cm[q], ix(cm_v, b)).then_inc(cm_loaded[q], 16)

            def load_seq(b):
                at_least(sp, seqm_ready, b)
                sp.dma_start(sm[:, :], seq_mask[bass.ds(b, 1), :].to_broadcast([P, S])).then_inc(sm_loaded, 16)

            def load_chunk(c, q):
                at_least(sp, wlo_ready, c - 1)
                sp.dma_start(stage[q][:, :], experts[bass.ds(c, 1)].rearrange("o p d -> (o p) d")
                             ).then_inc(w_loaded[q], 16)

            load_x(0, 0)
            sp.dma_start(wk[:, :, :], wk_t.rearrange("(c p) q -> p c q", p=P)).then_inc(consts_in, 16)
            sp.dma_start(col[:, :, :], cols).then_inc(consts_in, 16)
            sp.dma_start(bo[:, :], b_o.to_broadcast([P, D])).then_inc(consts_in, 16)
            load_ctx(0, 0)
            load_mask(0, 0)
            load_seq(0)
            load_x(1, 1)
            sp.dma_start(wo[:, :, :], wo_t.rearrange("(c p) o -> p c o", p=P)).then_inc(consts_in, 16)
            load_chunk(0, 0)
            load_chunk(1, 1)
            load_ctx(1, 1)
            load_mask(1, 1)
            load_chunk(2, 0)
            sp.wait_ge(consts_made, 3)
            third = ET // 3
            for i in range(3):
                sp.dma_start(disp_v[i * third:(i + 1) * third].rearrange("i p r -> p i r"),
                             pad_row.rearrange("p (o r) -> p o r", o=1).to_broadcast([P, third, ROW])
                             ).then_inc(pads_written, 16)
            sp.dma_start(out_v[T], rows[:, T - 1, 0:D]).then_inc(pads_written, 16)

            def loads(b, q):
                load_x(b + 2, q)
                if not isinstance(b, int) or b >= 1:
                    load_ctx(b + 1, 1 - q)
                    load_mask(b + 1, 1 - q)
                    load_seq(b + 1)
                    load_chunk(b + FIRST_CHUNKS - 1, q)

            loads(0, 0)
            load_seq(1)
            loads(1, 1)
            with sp.Fori(0, (B - 2 - 2) // 2) as turn:
                b = sp.snap(turn * 2 + 2)
                loads(b, 0)
                loads(b + 1, 1)
            for b in (B - 2, B - 1, B):
                if b + 1 < B:
                    load_ctx(b + 1, (b + 1) % 2)
                    load_mask(b + 1, (b + 1) % 2)
                    load_seq(b + 1)
                load_chunk(b + FIRST_CHUNKS - 1, b % 2)

            def store_shared(s, q):
                sp.wait_ge(y_ready, s + 1)
                sp.dma_start(ix(out_v, s), y[q]).then_inc(shared_stored[q], 16)

            c0 = FIRST_CHUNKS + CHUNKS_A
            for s in range(2):
                load_chunk(c0 + s, (c0 + s) % 2)
            load_chunk(c0 + 2, c0 % 2)
            store_shared(0, 0)
            with sp.Fori(0, (T - 3 - 1) // 2) as turn:
                s = sp.snap(turn * 2 + 1)
                load_chunk(s + c0 + 2, (c0 + 1) % 2)
                store_shared(s, 1)
                load_chunk(s + c0 + 3, c0 % 2)
                store_shared(s + 1, 0)
            load_chunk(T - 3 + c0 + 2, (c0 + 1) % 2)

            def load_rows(i, q):
                at_least(sp, h_ready, i + T - 3)
                sp.dma_start(xg[q], ix(disp_v, i)).then_inc(xg_loaded[q], 16)

            store_shared(T - 3, (T - 3) % 2)
            for i in range(2):
                sp.wait_ge(rows_sent[i], 16 * T)
            load_rows(0, 0)
            load_rows(1, 1)
            for s in (T - 2, T - 1):
                store_shared(s, s % 2)
            load_rows(2, 2)
            load_rows(3, 3)
            with sp.Fori(0, (ET - 3 - 4) // 4) as turn:
                i = sp.snap(turn * 4 + 4)
                for q in range(4):
                    load_rows(i + q, q)
            for i in range(ET - 3, ET):
                load_rows(i, i % 4)

        @block.gpsimd
        def _(pool):
            pool.sem_inc(row_ready, 1)
            pool.memset(tiny[:, :], TINY).then_inc(consts_made, 1)
            pool.memset(pad_row, 0.0).then_inc(tri_zero, 1)
            pool.wait_ge(tri_zero, 1)
            pool.iota(rows[:, T - 1, D + 1:D + 2].bitcast(I32), pattern=[[1, 1]], base=N, channel_multiplier=1
                      ).then_inc(consts_made, 1)
            pool.memset(ident[:, :], 0.0).then_inc(tri_zero, 1)
            pool.wait_ge(tri_zero, 2)
            pool.affine_select(out=ident[:, :], in_=ident[:, :], compare_op=ALU.not_equal, fill=1.0, base=0,
                               pattern=[[-1, P]], channel_multiplier=1).then_inc(consts_made, 1)

            def residual(b, q):
                pool.wait_ge(x_loaded[q], 8 * (b - q) + 16)
                pool.tensor_tensor(x1[:, bass.ds(b * QT, QT), :], x_in[q],
                                   bo[:, :].rearrange("p (o d) -> p o d", o=1).to_broadcast([P, QT, D]), ALU.add
                                   ).then_inc(xb_ready, 1)

            def keep_row(c):
                pool.wait_ge(xf_ready, c + 1)
                pool.tensor_copy(rows[:, bass.ds(c * QT, QT), 0:D], xf).then_inc(row_ready, 1)

            def masks(b, q):
                pool.wait_ge(logm_made, b + 1)
                alone(pool, pool_passed)
                pool.tensor_scalar(cm[q], cm[q], 0.0, MASKED, ALU.is_le, ALU.mult).then_inc(pen_ready, 1)
                pool.wait_ge(seqm_ready, b + 1)
                pool.wait_ge(pen_ready, b + 1)
                pool.tensor_tensor(log_m[:, :, :], log_m[:, :, :], cm[q], ALU.add).then_inc(pen_added, 1)
                pool.wait_ge(pen_added, b + 1)
                pool.tensor_tensor(log_m[:, :, :], log_m[:, :, :],
                                   sm_log[:, :].rearrange("p (o k) -> p o k", o=1).to_broadcast([P, QT, S]), ALU.add
                                   ).then_inc(logm_ready, 1)

            pool.wait_ge(consts_in, 64)
            residual(0, 0)
            pool.memset(ones, 1.0).then_inc(consts_made, 1)
            pool.memset(ones_b[:, :], 1.0).then_inc(consts_made, 1)
            pool.memset(before[:, :], 1.0).then_inc(tri_zero, 1)
            pool.wait_ge(tri_zero, 3)
            pool.affine_select(out=before[:, :], in_=before[:, :], compare_op=ALU.is_gt, fill=0.0, base=0,
                               pattern=[[1, P]], channel_multiplier=-1).then_inc(consts_made, 1)
            residual(1, 1)
            masks(0, 0)
            pool.iota(desc[:, :, :], pattern=[[-1, E], [0, T]], base=E, channel_multiplier=0,
                      allow_small_or_imprecise_dtypes=True).then_inc(consts_made, 1)
            pool.iota(tile_no[:, :, :], pattern=[[1, ET], [0, E]], base=0, channel_multiplier=0,
                      allow_small_or_imprecise_dtypes=True).then_inc(consts_made, 1)
            residual(2, 0)
            masks(1, 1)
            with pool.Fori(0, (B - 2 - 2) // 2) as turn:
                b = pool.snap(turn * 2 + 2)
                residual(b + 1, 1)
                masks(b, 0)
                keep_row(b - 2)
                residual(b + 2, 0)
                masks(b + 1, 1)
                keep_row(b - 1)
            residual(B - 1, 1)
            masks(B - 2, 0)
            keep_row(B - 4)
            masks(B - 1, 1)
            keep_row(B - 3)
            keep_row(B - 2)
            pool.wait_ge(pads_written, 64)
            pool.iota(rows[:, :, D + 1:D + 2].bitcast(I32), pattern=[[P, T], [1, 1]], base=0, channel_multiplier=1
                      ).then_inc(consts_made, 1)
            keep_row(B - 1)

            pool.wait_ge(consts_made, 9)
            pool.wait_ge(row_ready, B + 1)
            pool.wait_ge(pos_ready, 1)
            for k in range(TOP_K):
                pool.wait_ge(w_ready, k + 1)
                for t in range(T):
                    pool.indirect_dma_start(dispatch, bass.IndirectOffsetOnAxis(pos[k][:, t:t + 1], 0),
                                            rows[:, t, :], None).then_inc(rows_sent[k], 16)

            for i in range(2):
                pool.wait_ge(shared_stored[i], 16 * T // 2)

            def add_rows(i, q):
                pool.wait_ge(y_ready, i + T + 1)
                at_least(pool, added, 16 * i)
                alone(pool, pool_passed)
                pool.indirect_dma_start(out, bass.IndirectOffsetOnAxis(tok[:, q:q + 1], 0), y[q], None,
                                        compute_op=ALU.add).then_inc(added, 16)

            add_rows(0, 0)
            with pool.Fori(0, (ET - 2 - 1) // 4) as turn:
                i = pool.snap(turn * 4 + 1)
                for k in range(4):
                    add_rows(i + k, (1 + k) % 4)
            for i in range(ET - 2, ET):
                add_rows(i, i % 4)
            pool.wait_ge(added, 16 * ET)

        @block.scalar
        def _(act):
            act.preload_act_table_set("natural_log_exp_and_others")

            def split_hi(c, q):
                act.wait_ge(w_loaded[q], 8 * (c - q) + 16)
                act.activation(w_hi[:, bass.ds(c * CH, CH)], stage[q][:, :], ACT.Copy, scale=SW
                               ).then_inc(whi_ready, 1)

            def rough_rstd(n, a, z_):
                act.wait_ge(ve_ready, n)
                act.activation(r0[:, a:z_], ve[:, a:z_], ACT.Ln).then_inc(ln_ready, 1)
                act.wait_ge(ln_ready, n)
                act.activation(r0[:, a:z_], r0[:, a:z_], ACT.Exp, scale=-0.5).then_inc(r0_ready, 1)

            def exps(c, q):
                act.wait_ge(max_ready, c + 1)
                for t in range(QT):
                    e = act.activation(p[:, t, :], p[:, t, :], ACT.Exp, bias=nmax[:, t:t + 1],
                                       accum_out=sums[q][:, t:t + 1])
                e.then_inc(p_ready, 1)

            def k_out(b):
                act.wait_ge(k_done, b + 1)
                for m in range(DC):
                    e = act.activation(k_t[:, m, :], two(bank[1][:, :])[:, m, :], ACT.Identity, bias=col[:, m, 2:3])
                e.then_inc(kt_ready, 1)

            def x_out(b):
                act.wait_ge(tx_done, b + 1)
                act.activation(x_t, two(bank[0][:, :]), ACT.Copy).then_inc(xt_ready, 1)

            def p_out(c):
                act.wait_ge(tp_done, c + 1)
                act.activation(p_t, two(bank[3][:, :]), ACT.Copy).then_inc(pt_ready, 1)

            def a_out(c):
                act.wait_ge(a_done, c + 1)
                act.activation(a_t, two(bank[4][:, :]), ACT.Copy).then_inc(at_ready, 1)

            def xf_hi(c):
                act.wait_ge(txf_done, c + 1)
                act.activation(xt_hi[:, bass.ds(c * QT, QT), :, :],
                               bank[6][:, :].rearrange("p (t c q) -> p t c q", t=QT, c=DC), ACT.Copy, scale=SX
                               ).then_inc(xhi_ready, 1)

            def logs(b, q):
                act.wait_ge(cm_loaded[q], 8 * (b - q) + 16)
                at_least(act, s_masked, b)
                act.activation(log_m[:, :, :], cm[q], ACT.Ln, bias=tiny[:, :])
                at_least(act, logm_ready, b)
                act.wait_ge(sm_loaded, 16 * b + 16)
                act.activation(sm_log[:, :], sm[:, :], ACT.Ln, bias=tiny[:, :]).then_inc(logm_made, 1)

            act.wait_ge(consts_made, 3)
            rough_rstd(1, 2, 4)
            split_hi(0, 0)

            def step(b, q, first=False, last=False, chunk=True):
                s1 = not isinstance(b, int) or b < B
                s2 = not isinstance(b, int) or 1 <= b <= B
                s3 = not isinstance(b, int) or 2 <= b
                if s2:
                    exps(b - 1, 1 - q)
                if s1:
                    k_out(b)
                if s2:
                    p_out(b - 1)
                if s1:
                    x_out(b)
                if s2:
                    a_out(b - 1)
                if s3 or (isinstance(b, int) and b + 1 < B):
                    rough_rstd(b + 2, 0 if s3 else 2, 4 if (not isinstance(b, int) or b + 1 < B) else 2)
                if s1:
                    logs(b, q)
                if s3:
                    xf_hi(b - 2)
                if not isinstance(b, int) or 1 <= b <= CHUNKS_A:
                    split_hi(b + FIRST_CHUNKS - 1, q)

            step(0, 0)
            split_hi(1, 1)
            split_hi(2, 0)
            step(1, 1)
            with act.Fori(0, (B - 2 - 2) // 2) as turn:
                b = act.snap(turn * 2 + 2)
                step(b, 0)
                step(b + 1, 1)
            for b in range(B - 2, B + 2):
                step(b, b % 2)

            act.wait_ge(ve3_ready, 1)
            act.activation(r03, ve3, ACT.Ln).then_inc(ln_ready, 1)
            act.wait_ge(ln_ready, B + 4)
            act.activation(r03, r03, ACT.Exp, scale=-0.5).then_inc(r03_ready, 1)
            act.wait_ge(d_ready, 1)
            act.activation(expo, tmp, ACT.Exp).then_inc(expo_ready, 1)
            act.preload_act_table(ACT.Silu)

            def silu(n, q):
                act.wait_ge(g_done, n + 1)
                at_least(act, h_ready, n)
                act.activation(g_act, bank[2 * q][:, :], ACT.Silu, scale=1.0 / (SX * SW)).then_inc(act_ready, 1)

            def h_out(n):
                act.wait_ge(th_done, n + 1)
                at_least(act, d_done, n)
                act.activation(h_hi, bank[4][:, :], ACT.Copy).then_inc(hhi_ready, 1)

            def xe_out(i, q):
                act.wait_ge(tg_done, i + 1)
                act.activation(xe_hi[q], bank[6][:, 0:D].rearrange("p (c t) -> p c t", c=DC), ACT.Copy, scale=SX
                               ).then_inc(ghi_ready, 1)

            def y_out(n, r):
                act.wait_ge(d_done, n + 1)
                at_least(act, added, 16 * (n - T - 3))
                act.activation(y[r], bank[5][:, 0:D], ACT.Copy, scale=1.0 / (SH * SW)
                               ).then_inc(y_ready, 1)

            c0 = FIRST_CHUNKS + CHUNKS_A
            silu(0, 0)
            split_hi(c0, c0 % 2)
            def shared(s, q):
                h_out(s - 1)
                silu(s, q)
                split_hi(s + c0, (c0 + q) % 2)

            shared(1, 1)
            shared(2, 0)
            with act.Fori(0, (T - 1 - 3) // 2) as turn:
                s = act.snap(turn * 2 + 3)
                shared(s, 1)
                shared(s + 1, 0)
            h_out(T - 2)
            xe_out(0, 0)
            silu(T - 1, 1)
            split_hi(T - 1 + c0, (c0 + T - 1) % 2)

            def expert(i, k, more=True, y_too=True):
                h_out(i + T - 1)
                if more:
                    xe_out(i + 1, (k + 1) % 2)
                silu(i + T, k % 2)
                if y_too:
                    y_out(i + T - 1, (k + 3) % 4)

            expert(0, 0, y_too=False)
            act.wait_ge(shared_stored[0], 16 * T // 2)
            act.wait_ge(shared_stored[1], 16 * T // 2)
            for i in range(1, 5):
                expert(i, i % 4)
            with act.Fori(0, (ET - 2 - 5) // 4) as turn:
                i = act.snap(turn * 4 + 5)
                for k in range(4):
                    expert(i + k, (1 + k) % 4)
            expert(ET - 2, (ET - 2) % 4)
            expert(ET - 1, (ET - 1) % 4, more=False)
            h_out(ET + T - 1)
            y_out(ET + T - 1, (ET - 1) % 4)

        @block.vector
        def _(dve):
            def split_lo(c, q):
                dve.wait_ge(whi_ready, c + 1)
                dve.scalar_tensor_tensor(w_lo[:, bass.ds(c * CH, CH)], stage[q][:, :], SW,
                                         w_hi[:, bass.ds(c * CH, CH)], ALU.mult, ALU.subtract
                                         ).then_inc(wlo_ready, 1)

            def seq_penalty(b):
                dve.wait_ge(logm_made, b + 1)
                dve.tensor_scalar(sm[:, :], sm[:, :], 0.0, MASKED, ALU.is_le, ALU.mult).then_inc(smp_ready, 1)
                dve.wait_ge(smp_ready, b + 1)
                dve.tensor_tensor(sm_log[:, :], sm_log[:, :], sm[:, :], ALU.add).then_inc(seqm_ready, 1)

            def add_mask_and_max(c):
                dve.wait_ge(s_done, c + 1)
                dve.wait_ge(logm_ready, c + 1)
                at_least(dve, tp_done, c)
                dve.tensor_tensor(p, two(bank[2][:, :]), log_m[:, :, :], ALU.add).then_inc(s_masked, 1)
                dve.wait_ge(s_masked, c + 1)
                dve.tensor_reduce(nmax[:, :], p, AX.X, ALU.max, negate=True).then_inc(max_ready, 1)

            def norms(n, c, q1, b, q):
                a, z_ = (0 if c is not None else 2), (4 if b is not None else 2)
                if c is not None:
                    dve.wait_ge(p_ready, c + 1)
                    dve.reciprocal(rinv[:, :], sums[q1][:, :]).then_inc(rinv_ready, 1)
                    dve.wait_ge(rinv_ready, c + 1)
                    dve.wait_ge(o_done, c + 1)
                    dve.wait_ge(xb_ready, c + 1)
                    for t in range(QT):
                        i = dve.scalar_tensor_tensor(x1[:, bass.ds(c * QT + t, 1), :].rearrange("p o d -> p (o d)"),
                                                     two(bank[5][:, :])[:, t, :], rinv[:, t:t + 1],
                                                     x1[:, bass.ds(c * QT + t, 1), :].rearrange("p o d -> p (o d)"),
                                                     ALU.mult, ALU.add)
                    i.then_inc(x1_ready, 1)
                if b is not None:
                    dve.wait_ge(x_loaded[q], 8 * (b - q) + 16)
                    alone(dve, dve_passed)
                    for t in range(QT):
                        i = dve.bn_stats(stats[:, 2 + t, :], x_in[q][:, t, :])
                if c is not None:
                    dve.wait_ge(x1_ready, c + 1)
                    alone(dve, dve_passed)
                    for t in range(QT):
                        i = dve.bn_stats(stats[:, t, :], x1[:, bass.ds(c * QT + t, 1), :].rearrange("p o d -> p (o d)"))
                i.then_inc(stats_ready, 1)
                dve.wait_ge(stats_ready, n)
                alone(dve, dve_passed)
                for s in range(a, z_):
                    i = dve.bn_aggr(mv[:, s, :], stats[:, s, :])
                i.then_inc(mv_ready, 1)
                dve.wait_ge(mv_ready, n)
                v = ve[:, a:z_]
                dve.tensor_scalar(v, mv[:, a:z_, 1], LN_EPS, None, ALU.add).then_inc(ve_ready, 1)
                dve.wait_ge(r0_ready, n)
                r = r0[:, a:z_]
                newton(r, v, r2[:, a:z_], rstd[:, a:z_], nt_ready, 3 * (n - 1))
                if c is not None:
                    dve.wait_ge(row_ready, c + 1)
                    for t in range(QT):
                        i = dve.tensor_scalar(xf[:, t, :],
                                              x1[:, bass.ds(c * QT + t, 1), :].rearrange("p o d -> p (o d)"),
                                              mv[:, t, 0:1], rstd[:, t:t + 1], ALU.subtract, ALU.mult)
                    i.then_inc(xf_ready, 1)
                if b is not None:
                    at_least(dve, tx_done, b)
                    for t in range(QT):
                        i = dve.tensor_scalar(xln[:, t, :], x_in[q][:, t, :], mv[:, 2 + t, 0:1],
                                              rstd[:, 2 + t:3 + t], ALU.subtract, ALU.mult)
                    i.then_inc(xln_ready, 1)

            def newton(r, v, t2, res, chain, base):
                dve.tensor_tensor(t2, r, r, ALU.mult).then_inc(chain, 1)
                dve.wait_ge(chain, base + 1)
                dve.scalar_tensor_tensor(t2, t2, -0.5, v, ALU.mult, ALU.mult).then_inc(chain, 1)
                dve.wait_ge(chain, base + 2)
                dve.scalar_tensor_tensor(res, t2, 1.5, r, ALU.add, ALU.mult).then_inc(chain, 1)
                dve.wait_ge(chain, base + 3)

            def xf_stats_and_lo(c):
                dve.wait_ge(xf_ready, c + 1)
                alone(dve, dve_passed)
                for t in range(QT):
                    i = dve.bn_stats(stats3[:, t, :], xf[:, t, :])
                i.then_inc(st3_ready, 1)
                dve.wait_ge(st3_ready, c + 1)
                alone(dve, dve_passed)
                for t in range(QT):
                    i = dve.bn_aggr(mv_xf[:, t, :], stats3[:, t, :])
                i.then_inc(mvx_ready, 1)
                dve.wait_ge(mvx_ready, c + 1)
                dve.tensor_copy(mv3[:, bass.ds(c * QT, QT), :], mv_xf[:, :, :]).then_inc(mv3_ready, 1)
                dve.wait_ge(xhi_ready, c + 1)
                dve.scalar_tensor_tensor(xt_lo[:, bass.ds(c * QT, QT), :, :].rearrange("p t c q -> p (t c q)"),
                                         bank[6][:, :], SX,
                                         xt_hi[:, bass.ds(c * QT, QT), :, :].rearrange("p t c q -> p (t c q)"),
                                         ALU.mult, ALU.subtract).then_inc(xlo_ready, 1)

            norms(1, None, None, 0, 0)
            dve.wait_ge(consts_in, 64)
            for c in range(DC):
                dve.tensor_scalar(gate_bias[:, c, 0:E], col[:, c, 3:3 + E], col[:, c, 0:1], None, ALU.mult)
                i = dve.tensor_scalar(gate_bias[:, c, E:2 * E], col[:, c, 3:3 + E], col[:, c, 1:2], None, ALU.mult)
            i.then_inc(gates_made, 1)
            dve.wait_ge(gates_made, 1)
            dve.tensor_scalar(gate_hi[:, :, :], gate_bias[:, :, 0:E], SG, None, ALU.mult).then_inc(gates_made, 1)
            dve.wait_ge(gates_made, 2)
            dve.scalar_tensor_tensor(gate_lo[:, :, :], gate_bias[:, :, 0:E], SG, gate_hi[:, :, :],
                                     ALU.mult, ALU.subtract).then_inc(gates_made, 1)
            dve.wait_ge(gb_summed, 1)
            dve.tensor_copy(sg_c[:, :, :], bank[7][:, P:P + 2 * E].rearrange("p (a e) -> p a e", a=2)
                            ).then_inc(gb_copied, 1)
            split_lo(0, 0)

            def step(b, q):
                s2 = not isinstance(b, int) or 1 <= b <= B
                s3 = not isinstance(b, int) or 2 <= b
                nxt = not isinstance(b, int) or b + 1 < B
                if s2:
                    add_mask_and_max(b - 1)
                if s3 or nxt:
                    norms(b + 2, b - 2 if s3 else None, q, b + 1 if nxt else None, 1 - q)
                if not isinstance(b, int) or b < B:
                    seq_penalty(b)
                if s3:
                    xf_stats_and_lo(b - 2)
                if not isinstance(b, int) or 1 <= b <= CHUNKS_A:
                    split_lo(b + FIRST_CHUNKS - 1, q)

            step(0, 0)
            split_lo(1, 1)
            split_lo(2, 0)
            step(1, 1)
            with dve.Fori(0, (B - 2 - 2) // 2) as turn:
                b = dve.snap(turn * 2 + 2)
                step(b, 0)
                step(b + 1, 1)
            for b in range(B - 2, B + 2):
                step(b, b % 2)

            count = [0]

            def then(i):
                i.then_inc(route, 1)
                count[0] += 1
                dve.wait_ge(route, count[0])

            def over_experts(ap):
                return ap.rearrange("p (o t) -> p o t", o=1).to_broadcast([P, E, T])

            def over_tiles(ap):
                return ap.rearrange("p (e o) -> p e o", o=1).to_broadcast([P, E, T])

            dve.wait_ge(mv3_ready, B)
            dve.tensor_scalar(ve3, mv3[:, :, 1], LN_EPS, None, ALU.add).then_inc(ve3_ready, 1)
            dve.wait_ge(ve3_ready, 1)
            dve.wait_ge(r03_ready, 1)
            newton(r03, ve3, r23, rs3, route, count[0])
            count[0] += 3
            dve.scalar_tensor_tensor(nm3, mv3[:, :, 0], -1.0, rs3, ALU.mult, ALU.mult)
            then(dve.tensor_scalar(r23, rs3, 1.0 / (SX * SG), None, ALU.mult))
            dve.wait_ge(lg_done, B)
            dve.tensor_tensor(logit, bank[7][:, 0:P].rearrange("p (t e) -> p e t", e=E), over_experts(r23), ALU.mult)
            then(dve.tensor_tensor(tmp, over_tiles(sg_c[:, 0, :]), over_experts(nm3), ALU.mult))
            then(dve.tensor_tensor(logit, logit, tmp, ALU.add))
            then(dve.tensor_tensor(logit, logit, over_tiles(sg_c[:, 1, :]), ALU.add))
            then(dve.tensor_reduce(m1, by_tile(logit), AX.X, ALU.max))
            dve.tensor_tensor(tmp, logit, over_experts(m1), ALU.subtract).then_inc(d_ready, 1)
            then(dve.tensor_tensor(eq, logit, over_experts(m1), ALU.is_equal))
            dve.wait_ge(consts_made, 8)
            then(dve.tensor_tensor(eq, eq, desc[:, :, :], ALU.mult))
            then(dve.tensor_reduce(mx, by_tile(eq), AX.X, ALU.max))
            then(dve.tensor_tensor(one1, desc[:, :, :], over_experts(mx), ALU.is_equal))
            then(dve.scalar_tensor_tensor(logit, one1, -1e30, logit, ALU.mult, ALU.add))
            then(dve.tensor_reduce(m2, by_tile(logit), AX.X, ALU.max))
            then(dve.tensor_tensor(eq, logit, over_experts(m2), ALU.is_equal))
            then(dve.tensor_tensor(eq, eq, desc[:, :, :], ALU.mult))
            then(dve.tensor_reduce(mx, by_tile(eq), AX.X, ALU.max))
            then(dve.tensor_tensor(one2, desc[:, :, :], over_experts(mx), ALU.is_equal))
            dve.tensor_tensor(both[:, :, :], one1, one2, ALU.add).then_inc(both_ready, 1)
            dve.wait_ge(expo_ready, 1)
            then(dve.tensor_reduce(z, by_tile(expo), AX.X, ALU.add))
            then(dve.tensor_tensor(tmp, expo, one2, ALU.mult))
            then(dve.tensor_reduce(e2, by_tile(tmp), AX.X, ALU.add))
            then(dve.scalar_tensor_tensor(z, z, EPS, e2, ALU.mult, ALU.add))
            then(dve.tensor_scalar(z, z, 1.0, None, ALU.add))
            then(dve.reciprocal(w1, z))
            then(dve.tensor_tensor(w2, w1, e2, ALU.mult))
            dve.wait_ge(row_ready, B + 1)
            dve.tensor_scalar(rows[:, :, D], w1, SH / (SX * SW), None, ALU.mult).then_inc(w_ready, 1)
            then(dve.memset(zero_first, 1.0))
            dve.wait_ge(cum_done, 1)
            then(dve.tensor_copy(tmp, bank[7][:, 2 * P:3 * P].rearrange("p (e t) -> p e t", e=E)))
            then(dve.memset(zero_first[:, :, 0:1], 0.0))
            flat = lambda ap: ap.rearrange("p e t -> p (e t)")
            then(dve.tensor_tensor_scan(flat(cols_incl), flat(zero_first), flat(tmp), 0.0, ALU.mult, ALU.add))
            then(dve.tensor_tensor(offs, cols_incl, tmp, ALU.subtract))
            then(dve.tensor_scalar(n_int[:, 0, :], cols_incl[:, :, T - 1], float(P - 1), None, ALU.add))
            then(dve.tensor_scalar(n_int[:, 1, :], n_int[:, 0, :], 7, None, ALU.logical_shift_right))
            dve.memset(n_e[:, 2, :], 1.0)
            then(dve.tensor_copy(n_e[:, 0, :], n_int[:, 1, :]))
            then(dve.tensor_tensor_scan(n_e[:, 1, :], n_e[:, 2, :], n_e[:, 0, :], 0.0, ALU.mult, ALU.add))
            then(dve.tensor_tensor(n_e[:, 3, :], n_e[:, 1, :], n_e[:, 0, :], ALU.subtract))
            then(dve.tensor_scalar(n_e[:, 3, :], n_e[:, 3, :], float(P), None, ALU.mult))
            then(dve.tensor_tensor(offs, offs, over_tiles(n_e[:, 3, :]), ALU.add))
            then(dve.tensor_tensor(offs, offs, bank[7][:, 3 * P:4 * P].rearrange("p (e t) -> p e t", e=E), ALU.add))
            for k, one in enumerate((one1, one2)):
                then(dve.tensor_tensor(tmp, offs, one, ALU.mult))
                then(dve.tensor_reduce(posf[:, :], by_tile(tmp), AX.X, ALU.add))
                i = dve.tensor_copy(pos[k][:, :], posf[:, :])
                then(i)
            then(dve.tensor_tensor(te_cmp[:, :, :], tile_no[:, :, :],
                                   n_e[0:1, 1, :].rearrange("p (o e) -> p o e", o=1).to_broadcast([1, ET, E]), ALU.is_ge))
            then(dve.tensor_reduce(te_f[:, 0, :], te_cmp[:, :, :], AX.X, ALU.add))
            then(dve.tensor_scalar(te_f[:, 1, :], te_f[:, 0, :], float(E - 1), 3.0 * CH, ALU.min, ALU.mult))
            dve.tensor_scalar(te[:, :], te_f[:, 1, :], 3.0 * CH, None, ALU.add).then_inc(pos_ready, 1)

            def h_mul(n, q, scalar, row=None):
                dve.wait_ge(u_done, n + 1)
                dve.wait_ge(act_ready, n + 1)
                at_least(dve, th_done, n)
                if row is not None:
                    dve.tensor_copy(tok[:, row:row + 1], xg[row][:, D + 1:D + 2].bitcast(U32))
                dve.scalar_tensor_tensor(h, bank[2 * q + 1][:, :], scalar, g_act, ALU.mult, ALU.mult
                                         ).then_inc(h_ready, 1)

            def h_low(n):
                dve.wait_ge(hhi_ready, n + 1)
                dve.tensor_tensor(h_lo, bank[4][:, :], h_hi, ALU.subtract).then_inc(hlo_ready, 1)

            def xe_low(i, q):
                dve.wait_ge(ghi_ready, i + 1)
                dve.scalar_tensor_tensor(xe_lo[q], bank[6][:, 0:D].rearrange("p (c t) -> p c t", c=DC), SX, xe_hi[q],
                                         ALU.mult, ALU.subtract).then_inc(glo_ready, 1)

            def y_shared(s, q):
                dve.wait_ge(d_done, s + 1)
                at_least(dve, shared_stored[q], 8 * (s - q))
                dve.scalar_tensor_tensor(y[q], bank[5][:, 0:D], 1.0 / (SH * SW),
                                         x1[:, bass.ds(s, 1), :].rearrange("p o d -> p (o d)"), ALU.mult, ALU.add
                                         ).then_inc(y_ready, 1)

            shared_scale = SH / (SX * SW)
            c0 = FIRST_CHUNKS + CHUNKS_A

            def second_weights():
                dve.wait_ge(rows_sent[0], 16 * T)
                dve.tensor_scalar(rows[:, :, D], w2, SH / (SX * SW), None, ALU.mult).then_inc(w_ready, 1)

            def shared(s, q):
                h_low(s - 1)
                h_mul(s, q, shared_scale)
                y_shared(s - 1, 1 - q)
                split_lo(s + c0, (c0 + q) % 2)

            h_mul(0, 0, shared_scale)
            split_lo(c0, c0 % 2)
            shared(1, 1)
            shared(2, 0)
            with dve.Fori(0, (9 - 3) // 2) as turn:
                s = dve.snap(turn * 2 + 3)
                shared(s, 1)
                shared(s + 1, 0)
            second_weights()
            with dve.Fori(0, (T - 1 - 9) // 2) as turn:
                s = dve.snap(turn * 2 + 9)
                shared(s, 1)
                shared(s + 1, 0)
            h_low(T - 2)
            xe_low(0, 0)
            h_mul(T - 1, 1, shared_scale)
            y_shared(T - 2, 0)
            split_lo(T - 1 + c0, (c0 + T - 1) % 2)

            def expert(i, k, more=True):
                h_low(i + T - 1)
                if more:
                    xe_low(i + 1, (k + 1) % 2)
                at_least(dve, added, 16 * (i - 3))
                h_mul(i + T, k % 2, xg[k][:, D:D + 1], k)

            expert(0, 0)
            y_shared(T - 1, 1)
            for i in range(1, 5):
                expert(i, i % 4)
            with dve.Fori(0, (ET - 2 - 5) // 4) as turn:
                i = dve.snap(turn * 4 + 5)
                for k in range(4):
                    expert(i + k, (1 + k) % 4)
            expert(ET - 2, (ET - 2) % 4)
            expert(ET - 1, (ET - 1) % 4, more=False)
            h_low(ET + T - 1)

        @block.tensor
        def _(pe):
            pe.wait_ge(consts_made, 3)

            def transposes(dst, src):
                for c in range(2):
                    for t in range(2):
                        i = pe.transpose(dst[:, c, t * P:(t + 1) * P], src[:, t, c * P:(c + 1) * P], ident[:, :])
                return i

            def products(dst, lhs, rhs):
                for m in range(2):
                    for c in range(2):
                        i = pe.matmul(dst[:, m, :], lhs[:, c, m * P:(m + 1) * P], rhs[:, c, :],
                                      start=(c == 0), stop=(c == 1))
                return i

            def step(b, q):
                s1 = not isinstance(b, int) or b < B
                s2 = not isinstance(b, int) or 1 <= b <= B
                s3 = not isinstance(b, int) or 2 <= b
                if s1:
                    pe.wait_ge(dk_loaded[q], 8 * (b - q) + 16)
                    at_least(pe, kt_ready, b)
                    products(two(bank[1][:, :]), wk, c_dk[q]).then_inc(k_done, 1)
                if s2:
                    pe.wait_ge(p_ready, b)
                    at_least(pe, pt_ready, b - 1)
                    transposes(two(bank[3][:, :]), p).then_inc(tp_done, 1)
                if s1:
                    pe.wait_ge(xln_ready, b + 1)
                    at_least(pe, xt_ready, b)
                    transposes(two(bank[0][:, :]), xln).then_inc(tx_done, 1)
                if s2:
                    pe.wait_ge(pt_ready, b)
                    pe.wait_ge(kd_loaded[1 - q], 8 * (b - 1 - (1 - q)) + 16)
                    at_least(pe, at_ready, b - 1)
                    products(two(bank[4][:, :]), c_kd[1 - q], p_t).then_inc(a_done, 1)
                if s1:
                    pe.wait_ge(xt_ready, b + 1)
                    pe.wait_ge(kt_ready, b + 1)
                    at_least(pe, s_masked, b)
                    products(two(bank[2][:, :]), x_t, k_t).then_inc(s_done, 1)
                if s3:
                    pe.wait_ge(xf_ready, b - 1)
                    for t in range(QT):
                        for c in range(DC):
                            i = pe.transpose(bank[6][:, (t * DC + c) * P:(t * DC + c + 1) * P],
                                             xf[:, t, c * P:(c + 1) * P], ident[:, :])
                    i.then_inc(txf_done, 1)
                if s2:
                    pe.wait_ge(at_ready, b)
                    at_least(pe, x1_ready, b - 1)
                    products(two(bank[5][:, :]), a_t, wo).then_inc(o_done, 1)
                if s3:
                    pe.wait_ge(xlo_ready, b - 1)
                    for t in range(QT):
                        pair = [(xt_hi, gate_hi), (xt_hi, gate_lo), (xt_lo, gate_hi)]
                        for c in range(DC):
                            for j, (a, g) in enumerate(pair):
                                i = pe.matmul(bank[7][:, bass.ds((b * QT - 2 * QT + t) * E, E)],
                                              a[:, bass.ds(b * QT - 2 * QT + t, 1), c, :].rearrange("p o q -> p (o q)"),
                                              g[:, c, :], start=(c == 0 and j == 0), stop=(c == DC - 1 and j == 2))
                    i.then_inc(lg_done, 1)

            pe.wait_ge(consts_in, 64)
            pe.wait_ge(consts_made, 4)
            pe.wait_ge(gates_made, 3)
            for c in range(DC):
                i = pe.matmul(bank[7][:, P:P + 2 * E], ones, gate_bias[:, c, :], start=(c == 0), stop=(c == DC - 1))
            i.then_inc(gb_summed, 1)
            step(0, 0)
            step(1, 1)
            pe.wait_ge(gb_copied, 1)
            with pe.Fori(0, (B - 2) // 2) as turn:
                b = pe.snap(turn * 2 + 2)
                step(b, 0)
                step(b + 1, 1)
            step(B, 0)
            step(B + 1, 1)

            def three(dst, pairs, last):
                n = len(pairs)
                for j, (a_hi, a_lo, off, width) in enumerate(pairs):
                    for m, (a, w) in enumerate(((a_hi, w_hi), (a_hi, w_lo), (a_lo, w_hi))):
                        i = pe.matmul(dst, a, w[:, bass.ds(off, width)] if not isinstance(off, int)
                                      else w[:, off:off + width], start=(j == 0 and m == 0), stop=(j == n - 1 and m == 2))
                i.then_inc(last, 1)

            def gate_up(n, q, xh, xl, off, between):
                at_least(pe, act_ready, n - 1)
                three(bank[2 * q][:, :], [(xh(c), xl(c), off + c * I, I) for c in range(DC)], g_done)
                between()
                at_least(pe, h_ready, n - 1)
                three(bank[2 * q + 1][:, :], [(xh(c), xl(c), off + CH + c * I, I) for c in range(DC)], u_done)

            def h_trans(n):
                pe.wait_ge(h_ready, n + 1)
                at_least(pe, hlo_ready, n)
                for j in range(IC):
                    i = pe.transpose(bank[4][:, j * P:(j + 1) * P], h[:, j * P:(j + 1) * P], ident[:, :])
                i.then_inc(th_done, 1)

            def rows_trans(i_, k):
                pe.wait_ge(xg_loaded[k], 4 * (i_ - k) + 16)
                at_least(pe, glo_ready, i_)
                for c in range(DC):
                    i = pe.transpose(bank[6][:, c * P:(c + 1) * P], xg[k][:, c * P:(c + 1) * P], ident[:, :])
                i.then_inc(tg_done, 1)

            def down(n, off):
                pe.wait_ge(hlo_ready, n + 1)
                at_least(pe, y_ready, n)
                three(bank[5][:, 0:D],
                      [(h_hi[:, j * P:(j + 1) * P], h_lo[:, j * P:(j + 1) * P], off + 2 * CH + j * D, D)
                       for j in range(IC)], d_done)

            def shared(s, q, between):
                gate_up(s, q,
                        lambda c: xt_hi[:, bass.ds(s, 1), c, :].rearrange("p o q -> p (o q)"),
                        lambda c: xt_lo[:, bass.ds(s, 1), c, :].rearrange("p o q -> p (o q)"), 0, between)

            def count_rows():
                pe.wait_ge(both_ready, 1)
                pe.wait_ge(consts_made, 6)
                flat = both[:, :, :].rearrange("p e t -> p (e t)")
                pe.matmul(bank[7][:, 2 * P:3 * P], ones_b[:, :], flat, start=True, stop=True)
                pe.matmul(bank[7][:, 3 * P:4 * P], before[:, :], flat, start=True, stop=True).then_inc(cum_done, 1)

            pe.wait_ge(wlo_ready, FIRST_CHUNKS)
            shared(0, 0, count_rows)
            for s in range(1, 3):
                shared(s, s % 2, lambda: h_trans(s - 1))
                down(s - 1, 0)
            with pe.Fori(0, (T - 1 - 3) // 2) as turn:
                s = pe.snap(turn * 2 + 3)
                for k in range(2):
                    shared(s + k, (1 + k) % 2, lambda: h_trans(s + k - 1))
                    down(s + k - 1, 0)

            def last_between():
                h_trans(T - 2)
                rows_trans(0, 0)

            shared(T - 1, 1, last_between)
            down(T - 2, 0)

            pe.wait_ge(pos_ready, 1)
            pe.wait_ge(wlo_ready, 3 * (E + 1))

            def offset(i):
                return pe.value_load(te[0:1, bass.ds(i, 1)], min_val=3 * CH, max_val=3 * E * CH)

            def expert(i, k, prev_off, more=True):
                off = offset(i)
                pe.wait_ge(glo_ready, i + 1)

                def between():
                    h_trans(i + T - 1)
                    if more:
                        rows_trans(i + 1, (k + 1) % 4)
                gate_up(i + T, k % 2, lambda c: xe_hi[k % 2][:, c, :], lambda c: xe_lo[k % 2][:, c, :], off, between)
                down(i + T - 1, prev_off)
                return off

            off = 0
            for i in range(5):
                off = expert(i, i % 4, off)
            with pe.Fori(0, (ET - 2 - 5) // 4) as turn:
                i = pe.snap(turn * 4 + 5)
                off = offset(i - 1)
                for k in range(4):
                    off = expert(i + k, (1 + k) % 4, off)
            off = expert(ET - 2, (ET - 2) % 4, offset(ET - 3))
            off = expert(ET - 1, (ET - 1) % 4, off, more=False)
            h_trans(ET + T - 1)
            down(ET + T - 1, off)


def kernel(**inputs):
    import numpy as _np
    import concourse.bacc as _bacc
    from concourse import mybir as _mybir
    from concourse.bass_utils import run_bass_kernel_spmd as _run

    f = {k: _np.ascontiguousarray(v) for k, v in inputs.items()}
    pre = "L0_ffn_"

    def packed(w, c):
        w = w.reshape(-1, c, P, w.shape[-1])
        return w.transpose(0, 2, 1, 3).reshape(w.shape[0], P, -1)

    gate, up, down = (_np.concatenate([f[pre + "s" + n][None], f[pre + n]]) for n in ("Wg", "Wu", "Wd"))
    experts = _np.stack([packed(gate, DC), packed(up, DC), packed(down, IC)], axis=1).reshape(3 * (E + 1), P, CH)
    cols = _np.concatenate([f[pre + "ln_scale"][:, None], f[pre + "ln_bias"][:, None],
                            f["L0_xattn_b_k"][:, None], f[pre + "gate_w"].T], axis=1)
    arrays = {
        "x": f["x"].reshape(N, D),
        "ctx_kd": f["ctx_1024"],
        "ctx_dk": f["ctx_1024"].transpose(0, 2, 1),
        "cell_mask": f["mask_BxSxS2_ff1"],
        "seq_mask": f["mask_BxS2_ff1"],
        "wk_t": f["L0_xattn_W_k"].T,
        "wo_t": f["L0_xattn_W_o"].T,
        "b_o": f["L0_xattn_b_o"].reshape(1, D),
        "cols": cols.reshape(DC, P, 3 + E).transpose(1, 0, 2),
        "experts": experts,
    }
    arrays = {f"in_{k}_dram": _np.ascontiguousarray(v) for k, v in arrays.items()}
    nc = _bacc.Bacc("TRN2", target_bir_lowering=False, num_devices=1)
    args = [nc.dram_tensor(k, v.shape, _mybir.dt.from_np(v.dtype), kind="ExternalInput").ap()
            for k, v in arrays.items()]
    dispatch = nc.dram_tensor("dispatch", (ET * P, ROW), _mybir.dt.float32, kind="Internal").ap()
    out = nc.dram_tensor("out_0_dram", (N + P, D), _mybir.dt.float32, kind="ExternalOutput").ap()
    xattn_moe_kernel(nc, *args, dispatch, out)
    r = _run(nc, [arrays], core_ids=[0])
    return r.results[0]["out_0_dram"][:N].reshape(B, S, D)
```

```python
from contextlib import ExitStack

import concourse.bass as bass
from concourse import mybir
from concourse.alu_op_type import AluOpType as ALU

ACT = mybir.ActivationFunctionType
AX = mybir.AxisListType
F32 = mybir.dt.float32
F16 = mybir.dt.float16
BF16 = mybir.dt.bfloat16
I32 = mybir.dt.int32
U32 = mybir.dt.uint32

P = 128
B, S, D = 8, 256, 256
QT = S // P
DC = D // P
T = B * QT
N = B * S
E, TOP_K = 8, 2
I = 512
IC = I // P
CH = D * I // P
ET = N * TOP_K // P + E - 1
ROW = D + 2
LN_EPS = 1e-5
EPS = 1e-5
TINY = 2.0 ** -64
MASKED = -1e30

SX, SW, SG, SH = 2.0 ** 8, 2.0 ** 6, 2.0 ** 8, 4.0

CHUNKS_A = 9
FIRST_CHUNKS = 2
PADS = -(-ET // B)


def at_least(eng, sem, count):
    if not (isinstance(count, int) and count <= 0):
        eng.wait_ge(sem, count)


def alone(eng, passed):
    eng.sem_inc(passed, 1)


def xattn_moe_kernel(nc, x, ctx_kd, ctx_dk, cell_mask, seq_mask, wk_t, wo_t, b_o, cols, experts, dispatch, out):
    with ExitStack() as stack:
        def sb(name, shape, dt=F32):
            return stack.enter_context(nc.sbuf_tensor(name, shape, dt))

        def sem(name):
            return stack.enter_context(nc.semaphore(name))

        bank = [stack.enter_context(nc.psum_tensor(f"bank{i}", [P, 512], F32)) for i in range(8)]

        w_parts = sb("w_parts", [P, 2, 3 * (E + 1) * CH], F16)
        w_hi, w_lo = w_parts[:, 0, :], w_parts[:, 1, :]
        stage = [sb(f"stage{i}", [P, CH]) for i in range(2)]
        wk = sb("wk", [P, DC, D])
        wo = sb("wo", [P, DC, D])
        bo = sb("bo", [P, D])
        col = sb("col", [P, DC, 3 + E])
        gate_bias = sb("gate_bias", [P, DC, 2 * E])
        gate_s = sb("gate_s", [P, DC, E])
        gate_hi = sb("gate_hi", [P, DC, E], F16)
        gate_lo = sb("gate_lo", [P, DC, E], F16)
        ident = sb("ident", [P, P])
        ones_b = sb("ones_b", [P, P], BF16)
        before = sb("before", [P, P], BF16)
        desc = sb("desc", [P, E, T])
        tile_no = sb("tile_no", [1, ET, E], BF16)
        tiny = sb("tiny", [P, 1])

        x1 = sb("x1", [P, T, D])
        rows = sb("rows", [P, T, ROW])
        xt_hi = sb("xt_hi", [P, T, DC, P], F16)
        xt_lo = sb("xt_lo", [P, T, DC, P], F16)
        mv3 = sb("mv3", [P, T, 2])

        work = sb("work", [P, 15 * 512])
        slot = [work[:, i * 512:(i + 1) * 512] for i in range(15)]

        def two(ap):
            return ap.rearrange("p (t d) -> p t d", t=2)

        x_in = [two(slot[0]), two(slot[1])]
        c_kd = [two(slot[2]), two(slot[3])]
        c_dk = [two(slot[4]), two(slot[5])]
        cm = [two(slot[6]), two(slot[7])]
        xln, x_t, k_t, p, p_t, a_t, xf = [two(slot[i]) for i in range(8, 15)]
        log_m = sb("log_m", [P, QT, S])
        sm = sb("sm", [P, S])
        sm_log = sb("sm_log", [P, S])

        ones = slot[13][:, 0:P]
        pad_row = rows[:, T - 1, :]

        stats = sb("stats", [P, 4, 6])
        stats3 = sb("stats3", [P, 2, 6])
        mv_xf = sb("mv_xf", [P, QT, 2])
        mv = sb("mv", [P, 4, 2])
        ve = sb("ve", [P, 4])
        r0 = sb("r0", [P, 4])
        r2 = sb("r2", [P, 4])
        rstd = sb("rstd", [P, 4])
        nmax = sb("nmax", [P, QT])
        sums = [sb(f"sums{i}", [P, QT]) for i in range(2)]
        rinv = sb("rinv", [P, QT])

        xg = [slot[i][:, 0:ROW] for i in range(4)]
        g_act = slot[4]
        h = slot[5]
        h_hi = slot[6].bitcast(F16)[:, 0:I]
        h_lo = slot[6].bitcast(F16)[:, I:2 * I]
        xe_hi = [slot[7].bitcast(F16)[:, i * D:(i + 1) * D].rearrange("p (c t) -> p c t", c=DC) for i in range(2)]
        xe_lo = [slot[7].bitcast(F16)[:, (2 + i) * D:(3 + i) * D].rearrange("p (c t) -> p c t", c=DC) for i in range(2)]
        y = [slot[8 + i // 2][:, (i % 2) * D:(i % 2 + 1) * D] for i in range(4)]
        tok = sb("tok", [P, 4], U32)

        def et(i):
            return slot[10 + i // 4][:, (i % 4) * P:(i % 4 + 1) * P].rearrange("p (e t) -> p e t", e=E)

        def by_tile(ap):
            return ap.rearrange("p e t -> p t e")

        logit, eq, one1, one2, tmp, expo, cols_incl, offs, zero_first = [et(i) for i in range(9)]
        both = sb("both", [P, E, T], BF16)
        small = sb("small", [P, 12, T])
        ve3, r03, r23, rs3, nm3, m1, mx, m2, z, e2, w1, w2 = [small[:, i, :] for i in range(12)]
        sg_c = sb("sg_c", [P, 2, E])
        n_e = sb("n_e", [P, 4, E])
        n_int = sb("n_int", [P, 2, E], I32)
        posf = sb("posf", [P, T])
        pos = [sb(f"pos{i}", [P, T], U32) for i in range(2)]
        te_cmp = slot[13][0:1, 0:ET * E].rearrange("p (i e) -> p i e", e=E)
        te_f = slot[13][0:1, 320:320 + 2 * ET].rearrange("p (a i) -> p a i", a=2)
        te = sb("te", [1, ET], I32)

        wk_in, wo_in, cols_in = sem("wk_in"), sem("wo_in"), sem("cols_in")
        x_loaded = [sem(f"x_loaded{i}") for i in range(2)]
        kd_loaded = [sem(f"kd_loaded{i}") for i in range(2)]
        dk_loaded = [sem(f"dk_loaded{i}") for i in range(2)]
        cm_loaded = [sem(f"cm_loaded{i}") for i in range(2)]
        sm_loaded = sem("sm_loaded")
        w_loaded = [sem(f"w_loaded{i}") for i in range(2)]
        xg_loaded = [sem(f"xg_loaded{i}") for i in range(4)]
        pads_written = sem("pads_written")
        rows_sent = [sem(f"rows_sent{i}") for i in range(2)]
        shared_stored = [sem(f"shared_stored{i}") for i in range(2)]
        added = sem("added")
        consts_made = sem("consts_made")
        tri_zero = sem("tri_zero")
        gates_made = sem("gates_made")
        gb_summed, gb_copied = sem("gb_summed"), sem("gb_copied")
        xln_ready, tx_done, xt_ready = sem("xln_ready"), sem("tx_done"), sem("xt_ready")
        k_done, kt_ready, s_done = sem("k_done"), sem("kt_ready"), sem("s_done")
        xb_ready, logm_made, seqm_ready, pen_ready, logm_ready = (
            sem("xb_ready"), sem("logm_made"), sem("seqm_ready"), sem("pen_ready"), sem("logm_ready"))
        pen_added, smp_ready = sem("pen_added"), sem("smp_ready")
        s_masked, max_ready, p_ready = sem("s_masked"), sem("max_ready"), sem("p_ready")
        tp_done, pt_ready, a_done, at_ready, o_done = (
            sem("tp_done"), sem("pt_ready"), sem("a_done"), sem("at_ready"), sem("o_done"))
        rinv_ready, x1_ready = sem("rinv_ready"), sem("x1_ready")
        stats_ready, mv_ready, ve_ready, ln_ready, r0_ready, nt_ready = (
            sem("stats_ready"), sem("mv_ready"), sem("ve_ready"), sem("ln_ready"), sem("r0_ready"), sem("nt_ready"))
        dve_passed, pool_passed = sem("dve_passed"), sem("pool_passed")
        row_ready, mvx_ready = sem("row_ready"), sem("mvx_ready")
        xf_ready, st3_ready, mv3_ready, txf_done, xhi_ready, xlo_ready, lg_done = (
            sem("xf_ready"), sem("st3_ready"), sem("mv3_ready"), sem("txf_done"), sem("xhi_ready"),
            sem("xlo_ready"), sem("lg_done"))
        whi_ready, wlo_ready = sem("whi_ready"), sem("wlo_ready")
        route = sem("route")
        d_ready, expo_ready, ve3_ready, r03_ready, both_ready, cum_done, pos_ready = (
            sem("d_ready"), sem("expo_ready"), sem("ve3_ready"), sem("r03_ready"), sem("both_ready"),
            sem("cum_done"), sem("pos_ready"))
        w_ready = sem("w_ready")
        g_done, u_done, act_ready, h_ready, th_done, hhi_ready, hlo_ready, d_done, y_ready = (
            sem("g_done"), sem("u_done"), sem("act_ready"), sem("h_ready"), sem("th_done"), sem("hhi_ready"),
            sem("hlo_ready"), sem("d_done"), sem("y_ready"))
        tg_done, ghi_ready, glo_ready = sem("tg_done"), sem("ghi_ready"), sem("glo_ready")

        x_v = x.rearrange("(b t p) d -> b p t d", t=QT, p=P)
        kd_v = ctx_kd.rearrange("b (t p) d -> b p t d", p=P)
        dk_v = ctx_dk.rearrange("b (c p) k -> b p c k", p=P)
        cm_v = cell_mask.rearrange("b (t p) k -> b p t k", p=P)
        disp_v = dispatch.rearrange("(i p) r -> i p r", p=P)
        out_v = out.rearrange("(t p) d -> t p d", p=P)

        def ix(ap, i):
            return ap[bass.ds(i, 1)].rearrange("o p t d -> (o p) t d") if len(ap.shape) == 4 else \
                ap[bass.ds(i, 1)].rearrange("o p d -> (o p) d")

        block = stack.enter_context(nc.Block())

        @block.sync
        def _(sp):
            def load_x(b, q):
                at_least(sp, xln_ready, b - 1)
                at_least(sp, xb_ready, b - 1)
                sp.dma_start(x_in[q], ix(x_v, b)).then_inc(x_loaded[q], 16)

            def load_dk(b, q):
                at_least(sp, k_done, b - 1)
                sp.dma_start(c_dk[q], ix(dk_v, b)).then_inc(dk_loaded[q], 16)

            def load_kd(b, q):
                at_least(sp, a_done, b - 1)
                sp.dma_start(c_kd[q], ix(kd_v, b)).then_inc(kd_loaded[q], 16)

            def load_mask(b, q):
                at_least(sp, logm_ready, b - 1)
                sp.dma_start(cm[q], ix(cm_v, b)).then_inc(cm_loaded[q], 16)

            def load_seq(b):
                at_least(sp, seqm_ready, b)
                sp.dma_start(sm[:, :], seq_mask[bass.ds(b, 1), :].to_broadcast([P, S])).then_inc(sm_loaded, 16)

            def load_chunk(c, q):
                at_least(sp, wlo_ready, c - 1)
                sp.dma_start(stage[q][:, :], experts[bass.ds(c, 1)].rearrange("o p d -> (o p) d")
                             ).then_inc(w_loaded[q], 16)

            load_x(0, 0)
            load_dk(0, 0)
            sp.dma_start(wk[:, :, :], wk_t.rearrange("(c p) q -> p c q", p=P)).then_inc(wk_in, 16)
            load_mask(0, 0)
            load_seq(0)
            sp.dma_start(col[:, :, :], cols).then_inc(cols_in, 16)
            sp.dma_start(bo[:, :], b_o.to_broadcast([P, D])).then_inc(cols_in, 16)
            load_x(1, 1)
            load_dk(1, 1)
            load_kd(0, 0)
            load_mask(1, 1)
            load_chunk(0, 0)
            sp.dma_start(wo[:, :, :], wo_t.rearrange("(c p) o -> p c o", p=P)).then_inc(wo_in, 16)
            load_chunk(1, 1)
            load_kd(1, 1)
            sp.wait_ge(consts_made, 3)
            sp.dma_start(out_v[T], rows[:, T - 1, 0:D]).then_inc(pads_written, 16)

            def pad(b):
                sp.dma_start(disp_v[bass.ds(b * PADS, PADS)].rearrange("i p r -> p i r"),
                             pad_row.rearrange("p (o r) -> p o r", o=1).to_broadcast([P, PADS, ROW])
                             ).then_inc(pads_written, 16)

            def loads(b, q):
                if not isinstance(b, int) or b + 2 < B:
                    load_x(b + 2, q)
                if not isinstance(b, int) or 1 <= b < B - 1:
                    load_dk(b + 1, 1 - q)
                    load_mask(b + 1, 1 - q)
                load_chunk(b + FIRST_CHUNKS, q)
                if not isinstance(b, int) or b + 1 < B:
                    load_seq(b + 1)
                if not isinstance(b, int) or 1 <= b < B - 1:
                    load_kd(b + 1, 1 - q)
                pad(b)

            loads(0, 0)
            loads(1, 1)
            with sp.Fori(0, (B - 2 - 2) // 2) as turn:
                b = sp.snap(turn * 2 + 2)
                loads(b, 0)
                loads(b + 1, 1)
            loads(B - 2, 0)
            loads(B - 1, 1)
            load_chunk(B + FIRST_CHUNKS, B % 2)

            def store_shared(s, q):
                sp.wait_ge(y_ready, s + 1)
                sp.dma_start(ix(out_v, s), y[q]).then_inc(shared_stored[q], 16)

            c0 = FIRST_CHUNKS + CHUNKS_A
            load_chunk(c0, c0 % 2)
            load_chunk(c0 + 1, (c0 + 1) % 2)
            load_chunk(c0 + 2, c0 % 2)
            store_shared(0, 0)
            with sp.Fori(0, (T - 3 - 1) // 2) as turn:
                s = sp.snap(turn * 2 + 1)
                load_chunk(s + c0 + 2, (c0 + 1) % 2)
                store_shared(s, 1)
                load_chunk(s + c0 + 3, c0 % 2)
                store_shared(s + 1, 0)
            load_chunk(T - 3 + c0 + 2, (c0 + 1) % 2)

            def load_rows(i, q):
                at_least(sp, h_ready, i + T - 3)
                sp.dma_start(xg[q], ix(disp_v, i)).then_inc(xg_loaded[q], 16)

            store_shared(T - 3, (T - 3) % 2)
            for i in range(2):
                sp.wait_ge(rows_sent[i], 16 * T)
            load_rows(0, 0)
            load_rows(1, 1)
            for s in (T - 2, T - 1):
                store_shared(s, s % 2)
            load_rows(2, 2)
            load_rows(3, 3)
            with sp.Fori(0, (ET - 3 - 4) // 4) as turn:
                i = sp.snap(turn * 4 + 4)
                for q in range(4):
                    load_rows(i + q, q)
            for i in range(ET - 3, ET):
                load_rows(i, i % 4)

        @block.gpsimd
        def _(pool):
            pool.sem_inc(row_ready, 1)
            pool.memset(tiny[:, :], TINY).then_inc(consts_made, 1)
            pool.memset(pad_row, 0.0).then_inc(tri_zero, 1)
            pool.wait_ge(tri_zero, 1)
            pool.iota(rows[:, T - 1, D + 1:D + 2].bitcast(I32), pattern=[[1, 1]], base=N, channel_multiplier=1
                      ).then_inc(consts_made, 1)
            pool.memset(ident[:, :], 0.0).then_inc(tri_zero, 1)
            pool.wait_ge(tri_zero, 2)
            pool.affine_select(out=ident[:, :], in_=ident[:, :], compare_op=ALU.not_equal, fill=1.0, base=0,
                               pattern=[[-1, P]], channel_multiplier=1).then_inc(consts_made, 1)

            def residual(b, q):
                pool.wait_ge(x_loaded[q], 8 * (b - q) + 16)
                pool.tensor_tensor(x1[:, bass.ds(b * QT, QT), :], x_in[q],
                                   bo[:, :].rearrange("p (o d) -> p o d", o=1).to_broadcast([P, QT, D]), ALU.add
                                   ).then_inc(xb_ready, 1)

            def keep_row(c):
                pool.wait_ge(xf_ready, c + 1)
                pool.tensor_copy(rows[:, bass.ds(c * QT, QT), 0:D], xf).then_inc(row_ready, 1)

            def masks(b, q):
                pool.wait_ge(logm_made, b + 1)
                alone(pool, pool_passed)
                pool.tensor_scalar(cm[q], cm[q], 0.0, MASKED, ALU.is_le, ALU.mult).then_inc(pen_ready, 1)
                pool.wait_ge(seqm_ready, b + 1)
                pool.wait_ge(pen_ready, b + 1)
                pool.tensor_tensor(log_m[:, :, :], log_m[:, :, :], cm[q], ALU.add).then_inc(pen_added, 1)
                pool.wait_ge(pen_added, b + 1)
                pool.tensor_tensor(log_m[:, :, :], log_m[:, :, :],
                                   sm_log[:, :].rearrange("p (o k) -> p o k", o=1).to_broadcast([P, QT, S]), ALU.add
                                   ).then_inc(logm_ready, 1)

            pool.wait_ge(cols_in, 32)
            residual(0, 0)
            pool.memset(ones, 1.0).then_inc(consts_made, 1)
            pool.memset(ones_b[:, :], 1.0).then_inc(consts_made, 1)
            pool.memset(before[:, :], 1.0).then_inc(tri_zero, 1)
            pool.wait_ge(tri_zero, 3)
            pool.affine_select(out=before[:, :], in_=before[:, :], compare_op=ALU.is_gt, fill=0.0, base=0,
                               pattern=[[1, P]], channel_multiplier=-1).then_inc(consts_made, 1)
            residual(1, 1)
            masks(0, 0)
            pool.iota(desc[:, :, :], pattern=[[-1, E], [0, T]], base=E, channel_multiplier=0,
                      allow_small_or_imprecise_dtypes=True).then_inc(consts_made, 1)
            pool.iota(tile_no[:, :, :], pattern=[[1, ET], [0, E]], base=0, channel_multiplier=0,
                      allow_small_or_imprecise_dtypes=True).then_inc(consts_made, 1)
            residual(2, 0)
            masks(1, 1)
            with pool.Fori(0, (B - 2 - 2) // 2) as turn:
                b = pool.snap(turn * 2 + 2)
                residual(b + 1, 1)
                masks(b, 0)
                keep_row(b - 2)
                residual(b + 2, 0)
                masks(b + 1, 1)
                keep_row(b - 1)
            residual(B - 1, 1)
            masks(B - 2, 0)
            keep_row(B - 4)
            masks(B - 1, 1)
            keep_row(B - 3)
            keep_row(B - 2)
            pool.wait_ge(pads_written, 16 * (B + 1))
            pool.iota(rows[:, :, D + 1:D + 2].bitcast(I32), pattern=[[P, T], [1, 1]], base=0, channel_multiplier=1
                      ).then_inc(consts_made, 1)
            keep_row(B - 1)

            pool.wait_ge(consts_made, 9)
            pool.wait_ge(row_ready, B + 1)
            pool.wait_ge(pos_ready, 1)
            for k in range(TOP_K):
                pool.wait_ge(w_ready, k + 1)
                for t in range(T):
                    pool.indirect_dma_start(dispatch, bass.IndirectOffsetOnAxis(pos[k][:, t:t + 1], 0),
                                            rows[:, t, :], None).then_inc(rows_sent[k], 16)

            for i in range(2):
                pool.wait_ge(shared_stored[i], 16 * T // 2)

            def add_rows(i, q):
                pool.wait_ge(y_ready, i + T + 1)
                at_least(pool, added, 16 * i)
                alone(pool, pool_passed)
                pool.indirect_dma_start(out, bass.IndirectOffsetOnAxis(tok[:, q:q + 1], 0), y[q], None,
                                        compute_op=ALU.add).then_inc(added, 16)

            add_rows(0, 0)
            with pool.Fori(0, (ET - 2 - 1) // 4) as turn:
                i = pool.snap(turn * 4 + 1)
                for k in range(4):
                    add_rows(i + k, (1 + k) % 4)
            for i in range(ET - 2, ET):
                add_rows(i, i % 4)
            pool.wait_ge(added, 16 * ET)

        @block.scalar
        def _(act):
            act.preload_act_table_set("natural_log_exp_and_others")

            def split_hi(c, q):
                act.wait_ge(w_loaded[q], 8 * (c - q) + 16)
                act.activation(w_hi[:, bass.ds(c * CH, CH)], stage[q][:, :], ACT.Copy, scale=SW
                               ).then_inc(whi_ready, 1)

            def rough_rstd(n, a, z_):
                act.wait_ge(ve_ready, n)
                act.activation(r0[:, a:z_], ve[:, a:z_], ACT.Ln).then_inc(ln_ready, 1)
                act.wait_ge(ln_ready, n)
                act.activation(r0[:, a:z_], r0[:, a:z_], ACT.Exp, scale=-0.5).then_inc(r0_ready, 1)

            def exps(c, q):
                act.wait_ge(max_ready, c + 1)
                for t in range(QT):
                    e = act.activation(p[:, t, :], p[:, t, :], ACT.Exp, bias=nmax[:, t:t + 1],
                                       accum_out=sums[q][:, t:t + 1])
                e.then_inc(p_ready, 1)

            def k_out(b):
                act.wait_ge(k_done, b + 1)
                for m in range(DC):
                    e = act.activation(k_t[:, m, :], two(bank[1][:, :])[:, m, :], ACT.Identity, bias=col[:, m, 2:3])
                e.then_inc(kt_ready, 1)

            def x_out(b):
                act.wait_ge(tx_done, b + 1)
                act.activation(x_t, two(bank[0][:, :]), ACT.Copy).then_inc(xt_ready, 1)

            def p_out(c):
                act.wait_ge(tp_done, c + 1)
                act.activation(p_t, two(bank[3][:, :]), ACT.Copy).then_inc(pt_ready, 1)

            def a_out(c):
                act.wait_ge(a_done, c + 1)
                act.activation(a_t, two(bank[4][:, :]), ACT.Copy).then_inc(at_ready, 1)

            def xf_hi(c):
                act.wait_ge(txf_done, c + 1)
                act.activation(xt_hi[:, bass.ds(c * QT, QT), :, :],
                               bank[6][:, :].rearrange("p (t c q) -> p t c q", t=QT, c=DC), ACT.Copy, scale=SX
                               ).then_inc(xhi_ready, 1)

            def logs(b, q):
                act.wait_ge(cm_loaded[q], 8 * (b - q) + 16)
                at_least(act, s_masked, b)
                act.activation(log_m[:, :, :], cm[q], ACT.Ln, bias=tiny[:, :])
                at_least(act, logm_ready, b)
                act.wait_ge(sm_loaded, 16 * b + 16)
                act.activation(sm_log[:, :], sm[:, :], ACT.Ln, bias=tiny[:, :]).then_inc(logm_made, 1)

            act.wait_ge(consts_made, 3)
            rough_rstd(1, 2, 4)
            act.wait_ge(cols_in, 32)

            def step(b, q):
                reg = not isinstance(b, int)
                if reg or 3 <= b:
                    xf_hi(b - 3)
                if reg or b < B:
                    logs(b, q)
                if reg or 1 <= b <= B:
                    exps(b - 1, 1 - q)
                if reg or 1 <= b <= CHUNKS_A:
                    split_hi(b + FIRST_CHUNKS - 1, 1 - q)
                if reg or b < B + 2:
                    rough_rstd(b + 2, 0 if reg or b >= 2 else 2, 4 if reg or b + 1 < B else 2)
                if reg or 1 <= b <= B:
                    p_out(b - 1)
                if reg or b < B:
                    x_out(b)
                    k_out(b)
                if reg or 1 <= b <= B:
                    a_out(b - 1)

            step(0, 0)
            for c in range(FIRST_CHUNKS):
                split_hi(c, c)
            step(1, 1)
            step(2, 0)
            with act.Fori(0, (B - 1 - 3) // 2) as turn:
                b = act.snap(turn * 2 + 3)
                step(b, 1)
                step(b + 1, 0)
            for b in range(B - 1, B + 3):
                step(b, b % 2)

            act.wait_ge(ve3_ready, 1)
            act.activation(r03, ve3, ACT.Ln).then_inc(ln_ready, 1)
            act.wait_ge(ln_ready, B + 4)
            act.activation(r03, r03, ACT.Exp, scale=-0.5).then_inc(r03_ready, 1)
            act.wait_ge(d_ready, 1)
            act.activation(expo, tmp, ACT.Exp).then_inc(expo_ready, 1)
            act.preload_act_table(ACT.Silu)

            def silu(n, q):
                act.wait_ge(g_done, n + 1)
                at_least(act, h_ready, n)
                act.activation(g_act, bank[2 * q][:, :], ACT.Silu, scale=1.0 / (SX * SW)).then_inc(act_ready, 1)

            def h_out(n):
                act.wait_ge(th_done, n + 1)
                at_least(act, d_done, n)
                act.activation(h_hi, bank[4][:, :], ACT.Copy).then_inc(hhi_ready, 1)

            def xe_out(i, q):
                act.wait_ge(tg_done, i + 1)
                act.activation(xe_hi[q], bank[6][:, 0:D].rearrange("p (c t) -> p c t", c=DC), ACT.Copy, scale=SX
                               ).then_inc(ghi_ready, 1)

            def y_out(n, r):
                act.wait_ge(d_done, n + 1)
                at_least(act, added, 16 * (n - T - 3))
                act.activation(y[r], bank[5][:, 0:D], ACT.Copy, scale=1.0 / (SH * SW)
                               ).then_inc(y_ready, 1)

            c0 = FIRST_CHUNKS + CHUNKS_A
            silu(0, 0)
            split_hi(c0, c0 % 2)
            def shared(s, q):
                h_out(s - 1)
                silu(s, q)
                split_hi(s + c0, (c0 + q) % 2)

            shared(1, 1)
            shared(2, 0)
            with act.Fori(0, (T - 1 - 3) // 2) as turn:
                s = act.snap(turn * 2 + 3)
                shared(s, 1)
                shared(s + 1, 0)
            h_out(T - 2)
            xe_out(0, 0)
            silu(T - 1, 1)
            split_hi(T - 1 + c0, (c0 + T - 1) % 2)

            def expert(i, k, more=True, y_too=True):
                h_out(i + T - 1)
                if more:
                    xe_out(i + 1, (k + 1) % 2)
                silu(i + T, k % 2)
                if y_too:
                    y_out(i + T - 1, (k + 3) % 4)

            expert(0, 0, y_too=False)
            act.wait_ge(shared_stored[0], 16 * T // 2)
            act.wait_ge(shared_stored[1], 16 * T // 2)
            for i in range(1, 5):
                expert(i, i % 4)
            with act.Fori(0, (ET - 2 - 5) // 4) as turn:
                i = act.snap(turn * 4 + 5)
                for k in range(4):
                    expert(i + k, (1 + k) % 4)
            expert(ET - 2, (ET - 2) % 4)
            expert(ET - 1, (ET - 1) % 4, more=False)
            h_out(ET + T - 1)
            y_out(ET + T - 1, (ET - 1) % 4)

        @block.vector
        def _(dve):
            def split_lo(c, q):
                dve.wait_ge(whi_ready, c + 1)
                dve.scalar_tensor_tensor(w_lo[:, bass.ds(c * CH, CH)], stage[q][:, :], SW,
                                         w_hi[:, bass.ds(c * CH, CH)], ALU.mult, ALU.subtract
                                         ).then_inc(wlo_ready, 1)

            def seq_penalty(b):
                dve.wait_ge(logm_made, b + 1)
                dve.tensor_scalar(sm[:, :], sm[:, :], 0.0, MASKED, ALU.is_le, ALU.mult).then_inc(smp_ready, 1)
                dve.wait_ge(smp_ready, b + 1)
                dve.tensor_tensor(sm_log[:, :], sm_log[:, :], sm[:, :], ALU.add).then_inc(seqm_ready, 1)

            def add_mask_and_max(c):
                dve.wait_ge(s_done, c + 1)
                dve.wait_ge(logm_ready, c + 1)
                at_least(dve, tp_done, c)
                dve.tensor_tensor(p, two(bank[2][:, :]), log_m[:, :, :], ALU.add).then_inc(s_masked, 1)
                dve.wait_ge(s_masked, c + 1)
                dve.tensor_reduce(nmax[:, :], p, AX.X, ALU.max, negate=True).then_inc(max_ready, 1)

            def norms(n, c, q1, b, q, meanwhile=None):
                a, z_ = (0 if c is not None else 2), (4 if b is not None else 2)
                if b is not None:
                    dve.wait_ge(x_loaded[q], 8 * (b - q) + 16)
                    alone(dve, dve_passed)
                    for t in range(QT):
                        i = dve.bn_stats(stats[:, 2 + t, :], x_in[q][:, t, :])
                if c is not None:
                    dve.wait_ge(p_ready, c + 1)
                    dve.reciprocal(rinv[:, :], sums[q1][:, :]).then_inc(rinv_ready, 1)
                    dve.wait_ge(rinv_ready, c + 1)
                    dve.wait_ge(o_done, c + 1)
                    dve.wait_ge(xb_ready, c + 1)
                    for t in range(QT):
                        i = dve.scalar_tensor_tensor(x1[:, bass.ds(c * QT + t, 1), :].rearrange("p o d -> p (o d)"),
                                                     two(bank[5][:, :])[:, t, :], rinv[:, t:t + 1],
                                                     x1[:, bass.ds(c * QT + t, 1), :].rearrange("p o d -> p (o d)"),
                                                     ALU.mult, ALU.add)
                    i.then_inc(x1_ready, 1)
                if c is not None:
                    dve.wait_ge(x1_ready, c + 1)
                    alone(dve, dve_passed)
                    for t in range(QT):
                        i = dve.bn_stats(stats[:, t, :], x1[:, bass.ds(c * QT + t, 1), :].rearrange("p o d -> p (o d)"))
                i.then_inc(stats_ready, 1)
                dve.wait_ge(stats_ready, n)
                alone(dve, dve_passed)
                for s in range(a, z_):
                    i = dve.bn_aggr(mv[:, s, :], stats[:, s, :])
                i.then_inc(mv_ready, 1)
                dve.wait_ge(mv_ready, n)
                v = ve[:, a:z_]
                dve.tensor_scalar(v, mv[:, a:z_, 1], LN_EPS, None, ALU.add).then_inc(ve_ready, 1)
                if meanwhile is not None:
                    meanwhile()
                dve.wait_ge(r0_ready, n)
                r = r0[:, a:z_]
                newton(r, v, r2[:, a:z_], rstd[:, a:z_], nt_ready, 3 * (n - 1))
                if c is not None:
                    dve.wait_ge(row_ready, c + 1)
                    for t in range(QT):
                        i = dve.tensor_scalar(xf[:, t, :],
                                              x1[:, bass.ds(c * QT + t, 1), :].rearrange("p o d -> p (o d)"),
                                              mv[:, t, 0:1], rstd[:, t:t + 1], ALU.subtract, ALU.mult)
                    i.then_inc(xf_ready, 1)
                if b is not None:
                    at_least(dve, tx_done, b)
                    for t in range(QT):
                        i = dve.tensor_scalar(xln[:, t, :], x_in[q][:, t, :], mv[:, 2 + t, 0:1],
                                              rstd[:, 2 + t:3 + t], ALU.subtract, ALU.mult)
                    i.then_inc(xln_ready, 1)

            def newton(r, v, t2, res, chain, base):
                dve.tensor_tensor(t2, r, r, ALU.mult).then_inc(chain, 1)
                dve.wait_ge(chain, base + 1)
                dve.scalar_tensor_tensor(t2, t2, -0.5, v, ALU.mult, ALU.mult).then_inc(chain, 1)
                dve.wait_ge(chain, base + 2)
                dve.scalar_tensor_tensor(res, t2, 1.5, r, ALU.add, ALU.mult).then_inc(chain, 1)
                dve.wait_ge(chain, base + 3)

            def xf_stats(c):
                dve.wait_ge(xf_ready, c + 1)
                alone(dve, dve_passed)
                for t in range(QT):
                    i = dve.bn_stats(stats3[:, t, :], xf[:, t, :])
                i.then_inc(st3_ready, 1)
                dve.wait_ge(st3_ready, c + 1)
                alone(dve, dve_passed)
                for t in range(QT):
                    i = dve.bn_aggr(mv_xf[:, t, :], stats3[:, t, :])
                i.then_inc(mvx_ready, 1)
                dve.wait_ge(mvx_ready, c + 1)
                dve.tensor_copy(mv3[:, bass.ds(c * QT, QT), :], mv_xf[:, :, :]).then_inc(mv3_ready, 1)

            def xf_lo(c):
                dve.wait_ge(xhi_ready, c + 1)
                dve.scalar_tensor_tensor(xt_lo[:, bass.ds(c * QT, QT), :, :].rearrange("p t c q -> p (t c q)"),
                                         bank[6][:, :], SX,
                                         xt_hi[:, bass.ds(c * QT, QT), :, :].rearrange("p t c q -> p (t c q)"),
                                         ALU.mult, ALU.subtract).then_inc(xlo_ready, 1)

            norms(1, None, None, 0, 0)
            dve.wait_ge(cols_in, 32)
            for c in range(DC):
                dve.tensor_scalar(gate_bias[:, c, 0:E], col[:, c, 3:3 + E], col[:, c, 0:1], None, ALU.mult)
                i = dve.tensor_scalar(gate_bias[:, c, E:2 * E], col[:, c, 3:3 + E], col[:, c, 1:2], None, ALU.mult)
            i.then_inc(gates_made, 1)
            dve.wait_ge(gates_made, 1)
            dve.tensor_scalar(gate_hi[:, :, :], gate_bias[:, :, 0:E], SG, None, ALU.mult).then_inc(gates_made, 1)
            dve.wait_ge(gates_made, 2)
            dve.scalar_tensor_tensor(gate_lo[:, :, :], gate_bias[:, :, 0:E], SG, gate_hi[:, :, :],
                                     ALU.mult, ALU.subtract).then_inc(gates_made, 1)

            def step(b, q):
                reg = not isinstance(b, int)
                if reg or 1 <= b <= B:
                    add_mask_and_max(b - 1)
                if reg or 3 <= b:
                    xf_lo(b - 3)
                if reg or b < B + 2:
                    def meanwhile():
                        if reg or b < B:
                            seq_penalty(b)
                    norms(b + 2, b - 2 if reg or b >= 2 else None, q, b + 1 if reg or b + 1 < B else None, 1 - q,
                          meanwhile)
                if reg or 2 <= b < B + 2:
                    xf_stats(b - 2)
                if reg or 1 <= b <= CHUNKS_A:
                    split_lo(b + FIRST_CHUNKS - 1, 1 - q)

            step(0, 0)
            for c in range(FIRST_CHUNKS):
                split_lo(c, c)
            step(1, 1)
            dve.wait_ge(gb_summed, 1)
            dve.tensor_copy(sg_c[:, :, :], bank[7][:, P:P + 2 * E].rearrange("p (a e) -> p a e", a=2)
                            ).then_inc(gb_copied, 1)
            step(2, 0)
            with dve.Fori(0, (B - 1 - 3) // 2) as turn:
                b = dve.snap(turn * 2 + 3)
                step(b, 1)
                step(b + 1, 0)
            for b in range(B - 1, B + 3):
                step(b, b % 2)

            count = [0]

            def then(i):
                i.then_inc(route, 1)
                count[0] += 1
                dve.wait_ge(route, count[0])

            def over_experts(ap):
                return ap.rearrange("p (o t) -> p o t", o=1).to_broadcast([P, E, T])

            def over_tiles(ap):
                return ap.rearrange("p (e o) -> p e o", o=1).to_broadcast([P, E, T])

            dve.wait_ge(mv3_ready, B)
            dve.tensor_scalar(ve3, mv3[:, :, 1], LN_EPS, None, ALU.add).then_inc(ve3_ready, 1)
            dve.wait_ge(ve3_ready, 1)
            dve.wait_ge(r03_ready, 1)
            newton(r03, ve3, r23, rs3, route, count[0])
            count[0] += 3
            dve.scalar_tensor_tensor(nm3, mv3[:, :, 0], -1.0, rs3, ALU.mult, ALU.mult)
            then(dve.tensor_scalar(r23, rs3, 1.0 / (SX * SG), None, ALU.mult))
            dve.wait_ge(lg_done, B)
            dve.tensor_tensor(logit, bank[7][:, 0:P].rearrange("p (t e) -> p e t", e=E), over_experts(r23), ALU.mult)
            then(dve.tensor_tensor(tmp, over_tiles(sg_c[:, 0, :]), over_experts(nm3), ALU.mult))
            then(dve.tensor_tensor(logit, logit, tmp, ALU.add))
            then(dve.tensor_tensor(logit, logit, over_tiles(sg_c[:, 1, :]), ALU.add))
            then(dve.tensor_reduce(m1, by_tile(logit), AX.X, ALU.max))
            dve.tensor_tensor(tmp, logit, over_experts(m1), ALU.subtract).then_inc(d_ready, 1)
            then(dve.tensor_tensor(eq, logit, over_experts(m1), ALU.is_equal))
            dve.wait_ge(consts_made, 8)
            then(dve.tensor_tensor(eq, eq, desc[:, :, :], ALU.mult))
            then(dve.tensor_reduce(mx, by_tile(eq), AX.X, ALU.max))
            then(dve.tensor_tensor(one1, desc[:, :, :], over_experts(mx), ALU.is_equal))
            then(dve.scalar_tensor_tensor(logit, one1, -1e30, logit, ALU.mult, ALU.add))
            then(dve.tensor_reduce(m2, by_tile(logit), AX.X, ALU.max))
            then(dve.tensor_tensor(eq, logit, over_experts(m2), ALU.is_equal))
            then(dve.tensor_tensor(eq, eq, desc[:, :, :], ALU.mult))
            then(dve.tensor_reduce(mx, by_tile(eq), AX.X, ALU.max))
            then(dve.tensor_tensor(one2, desc[:, :, :], over_experts(mx), ALU.is_equal))
            dve.tensor_tensor(both[:, :, :], one1, one2, ALU.add).then_inc(both_ready, 1)
            dve.wait_ge(expo_ready, 1)
            then(dve.tensor_reduce(z, by_tile(expo), AX.X, ALU.add))
            then(dve.tensor_tensor(tmp, expo, one2, ALU.mult))
            then(dve.tensor_reduce(e2, by_tile(tmp), AX.X, ALU.add))
            then(dve.scalar_tensor_tensor(z, z, EPS, e2, ALU.mult, ALU.add))
            then(dve.tensor_scalar(z, z, 1.0, None, ALU.add))
            then(dve.reciprocal(w1, z))
            then(dve.tensor_tensor(w2, w1, e2, ALU.mult))
            dve.wait_ge(row_ready, B + 1)
            dve.tensor_scalar(rows[:, :, D], w1, SH / (SX * SW), None, ALU.mult).then_inc(w_ready, 1)
            then(dve.memset(zero_first, 1.0))
            dve.wait_ge(cum_done, 1)
            then(dve.tensor_copy(tmp, bank[7][:, 2 * P:3 * P].rearrange("p (e t) -> p e t", e=E)))
            then(dve.memset(zero_first[:, :, 0:1], 0.0))
            flat = lambda ap: ap.rearrange("p e t -> p (e t)")
            then(dve.tensor_tensor_scan(flat(cols_incl), flat(zero_first), flat(tmp), 0.0, ALU.mult, ALU.add))
            then(dve.tensor_tensor(offs, cols_incl, tmp, ALU.subtract))
            then(dve.tensor_scalar(n_int[:, 0, :], cols_incl[:, :, T - 1], float(P - 1), None, ALU.add))
            then(dve.tensor_scalar(n_int[:, 1, :], n_int[:, 0, :], 7, None, ALU.logical_shift_right))
            dve.memset(n_e[:, 2, :], 1.0)
            then(dve.tensor_copy(n_e[:, 0, :], n_int[:, 1, :]))
            then(dve.tensor_tensor_scan(n_e[:, 1, :], n_e[:, 2, :], n_e[:, 0, :], 0.0, ALU.mult, ALU.add))
            then(dve.tensor_tensor(n_e[:, 3, :], n_e[:, 1, :], n_e[:, 0, :], ALU.subtract))
            then(dve.tensor_scalar(n_e[:, 3, :], n_e[:, 3, :], float(P), None, ALU.mult))
            then(dve.tensor_tensor(offs, offs, over_tiles(n_e[:, 3, :]), ALU.add))
            then(dve.tensor_tensor(offs, offs, bank[7][:, 3 * P:4 * P].rearrange("p (e t) -> p e t", e=E), ALU.add))
            for k, one in enumerate((one1, one2)):
                then(dve.tensor_tensor(tmp, offs, one, ALU.mult))
                then(dve.tensor_reduce(posf[:, :], by_tile(tmp), AX.X, ALU.add))
                i = dve.tensor_copy(pos[k][:, :], posf[:, :])
                then(i)
            then(dve.tensor_tensor(te_cmp[:, :, :], tile_no[:, :, :],
                                   n_e[0:1, 1, :].rearrange("p (o e) -> p o e", o=1).to_broadcast([1, ET, E]), ALU.is_ge))
            then(dve.tensor_reduce(te_f[:, 0, :], te_cmp[:, :, :], AX.X, ALU.add))
            then(dve.tensor_scalar(te_f[:, 1, :], te_f[:, 0, :], float(E - 1), 3.0 * CH, ALU.min, ALU.mult))
            dve.tensor_scalar(te[:, :], te_f[:, 1, :], 3.0 * CH, None, ALU.add).then_inc(pos_ready, 1)

            def h_mul(n, q, scalar, row=None):
                dve.wait_ge(u_done, n + 1)
                dve.wait_ge(act_ready, n + 1)
                at_least(dve, th_done, n)
                if row is not None:
                    dve.tensor_copy(tok[:, row:row + 1], xg[row][:, D + 1:D + 2].bitcast(U32))
                dve.scalar_tensor_tensor(h, bank[2 * q + 1][:, :], scalar, g_act, ALU.mult, ALU.mult
                                         ).then_inc(h_ready, 1)

            def h_low(n):
                dve.wait_ge(hhi_ready, n + 1)
                dve.tensor_tensor(h_lo, bank[4][:, :], h_hi, ALU.subtract).then_inc(hlo_ready, 1)

            def xe_low(i, q):
                dve.wait_ge(ghi_ready, i + 1)
                dve.scalar_tensor_tensor(xe_lo[q], bank[6][:, 0:D].rearrange("p (c t) -> p c t", c=DC), SX, xe_hi[q],
                                         ALU.mult, ALU.subtract).then_inc(glo_ready, 1)

            def y_shared(s, q):
                dve.wait_ge(d_done, s + 1)
                at_least(dve, shared_stored[q], 8 * (s - q))
                dve.scalar_tensor_tensor(y[q], bank[5][:, 0:D], 1.0 / (SH * SW),
                                         x1[:, bass.ds(s, 1), :].rearrange("p o d -> p (o d)"), ALU.mult, ALU.add
                                         ).then_inc(y_ready, 1)

            shared_scale = SH / (SX * SW)
            c0 = FIRST_CHUNKS + CHUNKS_A

            def second_weights():
                dve.wait_ge(rows_sent[0], 16 * T)
                dve.tensor_scalar(rows[:, :, D], w2, SH / (SX * SW), None, ALU.mult).then_inc(w_ready, 1)

            def shared(s, q):
                h_low(s - 1)
                h_mul(s, q, shared_scale)
                y_shared(s - 1, 1 - q)
                split_lo(s + c0, (c0 + q) % 2)

            h_mul(0, 0, shared_scale)
            split_lo(c0, c0 % 2)
            shared(1, 1)
            shared(2, 0)
            with dve.Fori(0, (9 - 3) // 2) as turn:
                s = dve.snap(turn * 2 + 3)
                shared(s, 1)
                shared(s + 1, 0)
            second_weights()
            with dve.Fori(0, (T - 1 - 9) // 2) as turn:
                s = dve.snap(turn * 2 + 9)
                shared(s, 1)
                shared(s + 1, 0)
            h_low(T - 2)
            xe_low(0, 0)
            h_mul(T - 1, 1, shared_scale)
            y_shared(T - 2, 0)
            split_lo(T - 1 + c0, (c0 + T - 1) % 2)

            def expert(i, k, more=True):
                h_low(i + T - 1)
                if more:
                    xe_low(i + 1, (k + 1) % 2)
                at_least(dve, added, 16 * (i - 3))
                h_mul(i + T, k % 2, xg[k][:, D:D + 1], k)

            expert(0, 0)
            y_shared(T - 1, 1)
            for i in range(1, 5):
                expert(i, i % 4)
            with dve.Fori(0, (ET - 2 - 5) // 4) as turn:
                i = dve.snap(turn * 4 + 5)
                for k in range(4):
                    expert(i + k, (1 + k) % 4)
            expert(ET - 2, (ET - 2) % 4)
            expert(ET - 1, (ET - 1) % 4, more=False)
            h_low(ET + T - 1)

        @block.tensor
        def _(pe):
            pe.wait_ge(consts_made, 3)

            def transposes(dst, src):
                for c in range(2):
                    for t in range(2):
                        i = pe.transpose(dst[:, c, t * P:(t + 1) * P], src[:, t, c * P:(c + 1) * P], ident[:, :])
                return i

            def products(dst, lhs, rhs):
                for m in range(2):
                    for c in range(2):
                        i = pe.matmul(dst[:, m, :], lhs[:, c, m * P:(m + 1) * P], rhs[:, c, :],
                                      start=(c == 0), stop=(c == 1))
                return i

            def step(b, q):
                reg = not isinstance(b, int)
                s1, s2, s3, s4 = reg or b < B, reg or 1 <= b <= B, reg or 2 <= b <= B + 1, reg or 3 <= b
                if s4:
                    pe.wait_ge(xf_ready, b - 2)
                    for t in range(QT):
                        for c in range(DC):
                            i = pe.transpose(bank[6][:, (t * DC + c) * P:(t * DC + c + 1) * P],
                                             xf[:, t, c * P:(c + 1) * P], ident[:, :])
                    i.then_inc(txf_done, 1)
                if s3:
                    pe.wait_ge(at_ready, b - 1)
                    at_least(pe, x1_ready, b - 2)
                    products(two(bank[5][:, :]), a_t, wo).then_inc(o_done, 1)
                if s4:
                    pe.wait_ge(xlo_ready, b - 2)
                    for t in range(QT):
                        pair = [(xt_hi, gate_hi), (xt_hi, gate_lo), (xt_lo, gate_hi)]
                        for c in range(DC):
                            for j, (a, g) in enumerate(pair):
                                i = pe.matmul(bank[7][:, bass.ds((b * QT - 3 * QT + t) * E, E)],
                                              a[:, bass.ds(b * QT - 3 * QT + t, 1), c, :].rearrange("p o q -> p (o q)"),
                                              g[:, c, :], start=(c == 0 and j == 0), stop=(c == DC - 1 and j == 2))
                    i.then_inc(lg_done, 1)
                if s1:
                    pe.wait_ge(dk_loaded[q], 8 * (b - q) + 16)
                    at_least(pe, kt_ready, b)
                    products(two(bank[1][:, :]), wk, c_dk[q]).then_inc(k_done, 1)
                if s2:
                    pe.wait_ge(p_ready, b)
                    at_least(pe, pt_ready, b - 1)
                    transposes(two(bank[3][:, :]), p).then_inc(tp_done, 1)
                if s1:
                    pe.wait_ge(xln_ready, b + 1)
                    at_least(pe, xt_ready, b)
                    transposes(two(bank[0][:, :]), xln).then_inc(tx_done, 1)
                if s2:
                    pe.wait_ge(pt_ready, b)
                    pe.wait_ge(kd_loaded[1 - q], 8 * (b - 1 - (1 - q)) + 16)
                    at_least(pe, at_ready, b - 1)
                    products(two(bank[4][:, :]), c_kd[1 - q], p_t).then_inc(a_done, 1)
                if s1:
                    pe.wait_ge(xt_ready, b + 1)
                    pe.wait_ge(kt_ready, b + 1)
                    at_least(pe, s_masked, b)
                    products(two(bank[2][:, :]), x_t, k_t).then_inc(s_done, 1)

            pe.wait_ge(wk_in, 16)
            step(0, 0)
            pe.wait_ge(consts_made, 4)
            pe.wait_ge(gates_made, 3)
            for c in range(DC):
                i = pe.matmul(bank[7][:, P:P + 2 * E], ones, gate_bias[:, c, :], start=(c == 0), stop=(c == DC - 1))
            i.then_inc(gb_summed, 1)
            step(1, 1)
            pe.wait_ge(wo_in, 16)
            step(2, 0)
            pe.wait_ge(gb_copied, 1)
            with pe.Fori(0, (B - 1 - 3) // 2) as turn:
                b = pe.snap(turn * 2 + 3)
                step(b, 1)
                step(b + 1, 0)
            for b in range(B - 1, B + 3):
                step(b, b % 2)

            def three(dst, pairs, last):
                n = len(pairs)
                for j, (a_hi, a_lo, w) in enumerate(pairs):
                    for m, (a, part) in enumerate(((a_hi, 0), (a_hi, 1), (a_lo, 0))):
                        i = pe.matmul(dst, a, w[:, part, :], start=(j == 0 and m == 0), stop=(j == n - 1 and m == 2))
                i.then_inc(last, 1)

            def gate_up(n, q, xh, xl, w, between):
                at_least(pe, act_ready, n - 1)
                three(bank[2 * q][:, :], [(xh(c), xl(c), w[:, :, c * I:(c + 1) * I]) for c in range(DC)], g_done)
                between()
                at_least(pe, h_ready, n - 1)
                three(bank[2 * q + 1][:, :], 
                      [(xh(c), xl(c), w[:, :, CH + c * I:CH + (c + 1) * I]) for c in range(DC)], u_done)

            def h_trans(n):
                pe.wait_ge(h_ready, n + 1)
                at_least(pe, hlo_ready, n)
                for j in range(IC):
                    i = pe.transpose(bank[4][:, j * P:(j + 1) * P], h[:, j * P:(j + 1) * P], ident[:, :])
                i.then_inc(th_done, 1)

            def rows_trans(i_, k):
                pe.wait_ge(xg_loaded[k], 4 * (i_ - k) + 16)
                at_least(pe, glo_ready, i_)
                for c in range(DC):
                    i = pe.transpose(bank[6][:, c * P:(c + 1) * P], xg[k][:, c * P:(c + 1) * P], ident[:, :])
                i.then_inc(tg_done, 1)

            def down(n, w):
                pe.wait_ge(hlo_ready, n + 1)
                at_least(pe, y_ready, n)
                three(bank[5][:, 0:D],
                      [(h_hi[:, j * P:(j + 1) * P], h_lo[:, j * P:(j + 1) * P], 
                        w[:, :, 2 * CH + j * D:2 * CH + (j + 1) * D])
                       for j in range(IC)], d_done)

            w_shared = w_parts[:, :, 0:3 * CH]

            def shared(s, q, between):
                gate_up(s, q,
                        lambda c: xt_hi[:, bass.ds(s, 1), c, :].rearrange("p o q -> p (o q)"),
                        lambda c: xt_lo[:, bass.ds(s, 1), c, :].rearrange("p o q -> p (o q)"), w_shared, between)

            def count_rows():
                pe.wait_ge(both_ready, 1)
                pe.wait_ge(consts_made, 6)
                flat = both[:, :, :].rearrange("p e t -> p (e t)")
                pe.matmul(bank[7][:, 2 * P:3 * P], ones_b[:, :], flat, start=True, stop=True)
                pe.matmul(bank[7][:, 3 * P:4 * P], before[:, :], flat, start=True, stop=True).then_inc(cum_done, 1)

            pe.wait_ge(wlo_ready, 3)
            shared(0, 0, count_rows)
            for s in range(1, 3):
                shared(s, s % 2, lambda: h_trans(s - 1))
                down(s - 1, w_shared)
            with pe.Fori(0, (T - 1 - 3) // 2) as turn:
                s = pe.snap(turn * 2 + 3)
                for k in range(2):
                    shared(s + k, (1 + k) % 2, lambda: h_trans(s + k - 1))
                    down(s + k - 1, w_shared)

            def last_between():
                h_trans(T - 2)
                rows_trans(0, 0)

            shared(T - 1, 1, last_between)
            down(T - 2, w_shared)

            pe.wait_ge(pos_ready, 1)
            pe.wait_ge(wlo_ready, 3 * (E + 1))

            def weights(i):
                off = pe.value_load(te[0:1, bass.ds(i, 1)], min_val=3 * CH, max_val=3 * E * CH)
                return w_parts[:, :, bass.ds(off, 3 * CH)]

            def expert(i, k, w, w_before, more=True):
                pe.wait_ge(glo_ready, i + 1)

                def between():
                    h_trans(i + T - 1)
                    if more:
                        rows_trans(i + 1, (k + 1) % 4)
                gate_up(i + T, k % 2, lambda c: xe_hi[k % 2][:, c, :], lambda c: xe_lo[k % 2][:, c, :], w, between)
                w_last = w_before()
                w_next = weights(i + 1) if more else None
                down(i + T - 1, w_last)
                return w_next

            def experts_from(i, first, count, w, w_before, ends=False):
                for k in range(count):
                    w_next = expert(i + k, (first + k) % 4, w, w_before, more=not (ends and k == count - 1))
                    w_before, w = (lambda w=w: w), w_next
                return w_before

            experts_from(0, 0, 5, weights(0), lambda: w_shared)
            with pe.Fori(0, (ET - 2 - 5) // 4) as turn:
                i = pe.snap(turn * 4 + 5)
                experts_from(i, 1, 4, weights(i), lambda: weights(i - 1))
            w_before = experts_from(ET - 2, (ET - 2) % 4, 2, weights(ET - 2), lambda: weights(ET - 3), ends=True)
            h_trans(ET + T - 1)
            down(ET + T - 1, w_before())


def kernel(**inputs):
    import numpy as _np
    import concourse.bacc as _bacc
    from concourse import mybir as _mybir
    from concourse.bass_utils import run_bass_kernel_spmd as _run

    f = {k: _np.ascontiguousarray(v) for k, v in inputs.items()}
    pre = "L0_ffn_"

    def packed(w, c):
        w = w.reshape(-1, c, P, w.shape[-1])
        return w.transpose(0, 2, 1, 3).reshape(w.shape[0], P, -1)

    gate, up, down = (_np.concatenate([f[pre + "s" + n][None], f[pre + n]]) for n in ("Wg", "Wu", "Wd"))
    experts = _np.stack([packed(gate, DC), packed(up, DC), packed(down, IC)], axis=1).reshape(3 * (E + 1), P, CH)
    cols = _np.concatenate([f[pre + "ln_scale"][:, None], f[pre + "ln_bias"][:, None],
                            f["L0_xattn_b_k"][:, None], f[pre + "gate_w"].T], axis=1)
    arrays = {
        "x": f["x"].reshape(N, D),
        "ctx_kd": f["ctx_1024"],
        "ctx_dk": f["ctx_1024"].transpose(0, 2, 1),
        "cell_mask": f["mask_BxSxS2_ff1"],
        "seq_mask": f["mask_BxS2_ff1"],
        "wk_t": f["L0_xattn_W_k"].T,
        "wo_t": f["L0_xattn_W_o"].T,
        "b_o": f["L0_xattn_b_o"].reshape(1, D),
        "cols": cols.reshape(DC, P, 3 + E).transpose(1, 0, 2),
        "experts": experts,
    }
    arrays = {f"in_{k}_dram": _np.ascontiguousarray(v) for k, v in arrays.items()}
    nc = _bacc.Bacc("TRN2", target_bir_lowering=False, num_devices=1)
    args = [nc.dram_tensor(k, v.shape, _mybir.dt.from_np(v.dtype), kind="ExternalInput").ap()
            for k, v in arrays.items()]
    dispatch = nc.dram_tensor("dispatch", (B * PADS * P, ROW), _mybir.dt.float32, kind="Internal").ap()
    out = nc.dram_tensor("out_0_dram", (N + P, D), _mybir.dt.float32, kind="ExternalOutput").ap()
    xattn_moe_kernel(nc, *args, dispatch, out)
    r = _run(nc, [arrays], core_ids=[0])
    return r.results[0]["out_0_dram"][:N].reshape(B, S, D)
```

```python
from contextlib import ExitStack

import concourse.bass as bass
from concourse import mybir
from concourse.alu_op_type import AluOpType as ALU

ACT = mybir.ActivationFunctionType
AX = mybir.AxisListType
F32 = mybir.dt.float32
F16 = mybir.dt.float16
BF16 = mybir.dt.bfloat16
I32 = mybir.dt.int32
U32 = mybir.dt.uint32

P = 128
B, S, D = 8, 256, 256
QT = S // P
DC = D // P
T = B * QT
N = B * S
E, TOP_K = 8, 2
I = 512
IC = I // P
CH = D * I // P
ET = N * TOP_K // P + E - 1
ROW = D + 2
LN_EPS = 1e-5
EPS = 1e-5
TINY = 2.0 ** -64
MASKED = -1e30

SX, SW, SG, SH = 2.0 ** 8, 2.0 ** 6, 2.0 ** 8, 4.0

FIRST_CHUNKS = ((0,), (1, 2), (3, 4))
POOL_CHUNKS = range(5, 11)
C0 = POOL_CHUNKS.stop
ROUTED = 7
PADS = -(-ET // B)


assert T % 2 == 0 and B % 2 == 0 and (ET - 3) % 4 == 0 and (ET - 7) % 4 == 0
assert 3 * (E + 1) == C0 + 2 * (T - 1 - ROUTED)


def at_least(eng, sem, count):
    if not (isinstance(count, int) and count <= 0):
        eng.wait_ge(sem, count)


def alone(eng, passed):
    eng.sem_inc(passed, 1)


def xattn_moe_kernel(nc, x, ctx_kd, ctx_dk, cell_mask, seq_mask, wk_t, wo_t, b_o, cols, experts, dispatch, out):
    with ExitStack() as stack:
        def sb(name, shape, dt=F32):
            return stack.enter_context(nc.sbuf_tensor(name, shape, dt))

        def sem(name):
            return stack.enter_context(nc.semaphore(name))

        bank = [stack.enter_context(nc.psum_tensor(f"bank{i}", [P, 512], F32)) for i in range(8)]

        w_parts = sb("w_parts", [P, 2, 3 * (E + 1) * CH], F16)
        w_hi, w_lo = w_parts[:, 0, :], w_parts[:, 1, :]
        stage = [sb(f"stage{i}", [P, CH])[:, :] for i in range(2)]
        wk = sb("wk", [P, DC, D])
        wo = sb("wo", [P, DC, D])
        bo = sb("bo", [P, D])
        col = sb("col", [P, DC, 3 + E])
        gate_bias = sb("gate_bias", [P, DC, 2 * E])
        gate_hi = sb("gate_hi", [P, DC, E], F16)
        gate_lo = sb("gate_lo", [P, DC, E], F16)
        ident = sb("ident", [P, P])
        ones_b = sb("ones_b", [P, P], BF16)
        before = sb("before", [P, P], BF16)
        desc = sb("desc", [P, E, T])
        tile_no = sb("tile_no", [1, ET, E], BF16)
        tiny = sb("tiny", [P, 1])

        x1 = sb("x1", [P, T, D])
        rows = sb("rows", [P, T, ROW])
        xt = sb("xt", [P, T, 2, DC, P], F16)
        mv3 = sb("mv3", [P, T, 2])

        work = sb("work", [P, 15 * 512])
        slot = [work[:, i * 512:(i + 1) * 512] for i in range(15)]

        def two(ap):
            return ap.rearrange("p (t d) -> p t d", t=2)

        x_in = [two(slot[0]), two(slot[1])]
        c_kd = [two(slot[2]), two(slot[3])]
        c_dk = [two(slot[4]), two(slot[5])]
        cm = [two(slot[6]), two(slot[7])]
        xln, x_t, k_t, p, p_t, a_t, xf = [two(slot[i]) for i in range(8, 15)]
        stage += [work[:, i * CH:(i + 1) * CH] for i in range(2)]
        stages = (2, 3, 1, 0)
        log_m = sb("log_m", [P, QT, S])
        sm = sb("sm", [P, S])
        sm_log = sb("sm_log", [P, S])

        ones = slot[13][:, 0:P]
        pad_row = rows[:, T - 1, :]

        stats = sb("stats", [P, 4, 6])
        stats3 = sb("stats3", [P, 2, 6])
        mv_xf = sb("mv_xf", [P, QT, 2])
        mv = sb("mv", [P, 4, 2])
        ve = sb("ve", [P, 4])
        r0 = sb("r0", [P, 4])
        r2 = sb("r2", [P, 4])
        rstd = sb("rstd", [P, 4])
        nmax = sb("nmax", [P, QT])
        sums = [sb(f"sums{i}", [P, QT]) for i in range(2)]
        rinv = sb("rinv", [P, QT])

        xg = [slot[i][:, 0:ROW] for i in range(4)]
        g_act = slot[4]
        h = slot[5]
        h_hi = slot[6].bitcast(F16)[:, 0:I]
        h_lo = slot[6].bitcast(F16)[:, I:2 * I]
        xe_hi = [slot[7].bitcast(F16)[:, i * D:(i + 1) * D].rearrange("p (c t) -> p c t", c=DC) for i in range(2)]
        xe_lo = [slot[7].bitcast(F16)[:, (2 + i) * D:(3 + i) * D].rearrange("p (c t) -> p c t", c=DC) for i in range(2)]
        y = [slot[8 + i // 2][:, (i % 2) * D:(i % 2 + 1) * D] for i in range(4)]
        tok = sb("tok", [P, 4], U32)

        def et(i):
            return slot[10 + i // 4][:, (i % 4) * P:(i % 4 + 1) * P].rearrange("p (e t) -> p e t", e=E)

        def by_tile(ap):
            return ap.rearrange("p e t -> p t e")

        logit, eq, one1, one2, tmp, expo, cols_incl, offs, zero_first = [et(i) for i in range(9)]
        both = sb("both", [P, E, T], BF16)
        small = sb("small", [P, 12, T])
        ve3, r03, r23, rs3, nm3, m1, mx, m2, z, e2, w1, w2 = [small[:, i, :] for i in range(12)]
        sg_c = sb("sg_c", [P, 2, E])
        n_e = sb("n_e", [P, 4, E])
        n_int = sb("n_int", [P, 2, E], I32)
        posf = small[:, 3:5, :]
        pos = [sb(f"pos{i}", [P, T], U32) for i in range(2)]
        te_cmp = slot[13][0:1, 0:ET * E].rearrange("p (i e) -> p i e", e=E)
        te_f = slot[13][0:1, 320:320 + 2 * ET].rearrange("p (a i) -> p a i", a=2)
        te = sb("te", [1, ET], I32)

        wk_in, wo_in, cols_in = sem("wk_in"), sem("wo_in"), sem("cols_in")
        x_loaded = [sem(f"x_loaded{i}") for i in range(2)]
        kd_loaded = [sem(f"kd_loaded{i}") for i in range(2)]
        dk_loaded = [sem(f"dk_loaded{i}") for i in range(2)]
        cm_loaded = [sem(f"cm_loaded{i}") for i in range(2)]
        sm_loaded = sem("sm_loaded")
        w_loaded = [sem(f"w_loaded{i}") for i in range(2)]
        late_loaded = [sem(f"late_loaded{i}") for i in range(4)]
        xg_loaded = [sem(f"xg_loaded{i}") for i in range(4)]
        pads_written = sem("pads_written")
        rows_sent = [sem(f"rows_sent{i}") for i in range(4)]
        shared_stored = [sem(f"shared_stored{i}") for i in range(2)]
        added = sem("added")
        consts_made = sem("consts_made")
        tri_zero = sem("tri_zero")
        gates_made = sem("gates_made")
        gb_summed, gb_copied = sem("gb_summed"), sem("gb_copied")
        xln_ready, tx_done, xt_ready = sem("xln_ready"), sem("tx_done"), sem("xt_ready")
        k_done, kt_ready, s_done = sem("k_done"), sem("kt_ready"), sem("s_done")
        xb_ready, logm_made, seqm_ready, pen_ready, logm_ready = (
            sem("xb_ready"), sem("logm_made"), sem("seqm_ready"), sem("pen_ready"), sem("logm_ready"))
        pen_added, smp_ready = sem("pen_added"), sem("smp_ready")
        s_masked, max_ready, p_ready = sem("s_masked"), sem("max_ready"), sem("p_ready")
        tp_done, pt_ready, a_done, at_ready, o_done = (
            sem("tp_done"), sem("pt_ready"), sem("a_done"), sem("at_ready"), sem("o_done"))
        rinv_ready, x1_ready = sem("rinv_ready"), sem("x1_ready")
        stats_ready, mv_ready, ve_ready, ln_ready, r0_ready, nt_ready = (
            sem("stats_ready"), sem("mv_ready"), sem("ve_ready"), sem("ln_ready"), sem("r0_ready"), sem("nt_ready"))
        dve_passed, pool_passed = sem("dve_passed"), sem("pool_passed")
        row_ready, mvx_ready = sem("row_ready"), sem("mvx_ready")
        xf_ready, st3_ready, mv3_ready, txf_done, xhi_ready, xlo_ready, lg_done = (
            sem("xf_ready"), sem("st3_ready"), sem("mv3_ready"), sem("txf_done"), sem("xhi_ready"),
            sem("xlo_ready"), sem("lg_done"))
        whi_ready, wlo_ready, pool_split = sem("whi_ready"), sem("wlo_ready"), sem("pool_split")
        route = sem("route")
        d_ready, expo_ready, ve3_ready, r03_ready, both_ready, cum_done, pos_ready = (
            sem("d_ready"), sem("expo_ready"), sem("ve3_ready"), sem("r03_ready"), sem("both_ready"),
            sem("cum_done"), sem("pos_ready"))
        w_ready = sem("w_ready")
        g_done, u_done, act_ready, h_ready, th_done, hhi_ready, hlo_ready, d_done, y_ready = (
            sem("g_done"), sem("u_done"), sem("act_ready"), sem("h_ready"), sem("th_done"), sem("hhi_ready"),
            sem("hlo_ready"), sem("d_done"), sem("y_ready"))
        tg_done, ghi_ready, glo_ready = sem("tg_done"), sem("ghi_ready"), sem("glo_ready")

        x_v = x.rearrange("(b t p) d -> b p t d", t=QT, p=P)
        kd_v = ctx_kd.rearrange("b (t p) d -> b p t d", p=P)
        dk_v = ctx_dk.rearrange("b (c p) k -> b p c k", p=P)
        cm_v = cell_mask.rearrange("b (t p) k -> b p t k", p=P)
        disp_v = dispatch.rearrange("(i p) r -> i p r", p=P)
        out_v = out.rearrange("(t p) d -> t p d", p=P)

        def ix(ap, i):
            return ap[bass.ds(i, 1)].rearrange("o p t d -> (o p) t d") if len(ap.shape) == 4 else \
                ap[bass.ds(i, 1)].rearrange("o p d -> (o p) d")

        block = stack.enter_context(nc.Block())

        @block.sync
        def _(sp):
            def load_x(b, q):
                at_least(sp, xln_ready, b - 1)
                at_least(sp, xb_ready, b - 1)
                sp.dma_start(x_in[q], ix(x_v, b)).then_inc(x_loaded[q], 16)

            def load_dk(b, q):
                at_least(sp, k_done, b - 1)
                sp.dma_start(c_dk[q], ix(dk_v, b)).then_inc(dk_loaded[q], 16)

            def load_kd(b, q):
                at_least(sp, a_done, b - 1)
                sp.dma_start(c_kd[q], ix(kd_v, b)).then_inc(kd_loaded[q], 16)

            def load_mask(b, q):
                at_least(sp, logm_ready, b - 1)
                sp.dma_start(cm[q], ix(cm_v, b)).then_inc(cm_loaded[q], 16)

            def load_seq(b):
                at_least(sp, seqm_ready, b)
                sp.dma_start(sm[:, :], seq_mask[bass.ds(b, 1), :].to_broadcast([P, S])).then_inc(sm_loaded, 16)

            def load_chunk(c, q):
                at_least(sp, wlo_ready, c - 1)
                sp.dma_start(stage[q], experts[bass.ds(c, 1)].rearrange("o p d -> (o p) d")
                             ).then_inc(w_loaded[q], 16)

            load_x(0, 0)
            load_dk(0, 0)
            sp.dma_start(wk[:, :, :], wk_t.rearrange("(c p) q -> p c q", p=P)).then_inc(wk_in, 16)
            load_mask(0, 0)
            load_seq(0)
            sp.dma_start(col[:, :, :], cols).then_inc(cols_in, 16)
            sp.dma_start(bo[:, :], b_o.to_broadcast([P, D])).then_inc(cols_in, 16)
            load_x(1, 1)
            load_dk(1, 1)
            load_kd(0, 0)
            load_mask(1, 1)
            load_chunk(0, 0)
            sp.dma_start(wo[:, :, :], wo_t.rearrange("(c p) o -> p c o", p=P)).then_inc(wo_in, 16)
            load_chunk(1, 1)
            load_kd(1, 1)
            sp.wait_ge(consts_made, 3)
            sp.dma_start(out_v[T], rows[:, T - 1, 0:D]).then_inc(pads_written, 16)

            def pad(b):
                sp.dma_start(disp_v[bass.ds(b * PADS, PADS)].rearrange("i p r -> p i r"),
                             pad_row.rearrange("p (o r) -> p o r", o=1).to_broadcast([P, PADS, ROW])
                             ).then_inc(pads_written, 16)

            def loads(b, q):
                if not isinstance(b, int) or b + 2 < B:
                    load_x(b + 2, q)
                if not isinstance(b, int) or b + 1 < B:
                    load_dk(b + 1, 1 - q)
                    load_mask(b + 1, 1 - q)
                    load_seq(b + 1)
                    load_kd(b + 1, 1 - q)
                pad(b)

            load_seq(1)
            load_x(2, 0)
            load_chunk(2, 0)
            pad(0)
            loads(1, 1)
            load_chunk(3, 1)
            load_chunk(4, 0)
            with sp.Fori(0, (B - 2 - 2) // 2) as turn:
                b = sp.snap(turn * 2 + 2)
                loads(b, 0)
                loads(b + 1, 1)
            loads(B - 2, 0)
            load_chunk(5, 1)
            load_chunk(6, 0)
            loads(B - 1, 1)

            def load_for_pool(c):
                sp.wait_ge(pool_split, c - POOL_CHUNKS.start - 1)
                sp.dma_start(stage[c % 2], experts[c]).then_inc(w_loaded[c % 2], 16)

            load_for_pool(7)
            load_for_pool(8)

            def store_shared(s, q):
                sp.wait_ge(y_ready, s + 1)
                sp.dma_start(ix(out_v, s), y[q]).then_inc(shared_stored[q], 16)

            def load_late(t, m):
                if not isinstance(t, int):
                    sp.wait_ge(wlo_ready, POOL_CHUNKS.start + 4 * t + m - 3)
                sp.dma_start(stage[stages[m]], experts[bass.ds(C0 + 4 * t + m, 1)].rearrange("o p d -> (o p) d")
                             ).then_inc(late_loaded[m], 16)

            sp.wait_ge(xln_ready, B)
            sp.wait_ge(xb_ready, B)
            sp.wait_ge(a_done, B)
            load_late(0, 0)
            load_late(0, 1)
            load_for_pool(9)
            for s in range(ROUTED - 2):
                store_shared(s, s % 2)
                if s == 1:
                    load_for_pool(10)
            for m in (2, 3):
                sp.wait_ge(pool_split, len(POOL_CHUNKS) + m - 3)
                load_late(0, m)
            store_shared(ROUTED - 2, (ROUTED - 2) % 2)
            with sp.Fori(1, (T - 1 - ROUTED) // 2) as turn:
                t = sp.snap(turn)
                for k in range(2):
                    store_shared(2 * t + ROUTED - 3 + k, (ROUTED - 1 + k) % 2)
                    load_late(t, 2 * k)
                    load_late(t, 2 * k + 1)
            store_shared(T - 4, (T - 4) % 2)

            def load_rows(i, q):
                if not isinstance(i, int) or i >= 4:
                    sp.wait_ge(h_ready, i + T - 3)
                sp.dma_start(xg[q], ix(disp_v, i)).then_inc(xg_loaded[q], 16)

            for i in range(4):
                sp.wait_ge(rows_sent[i], 16 * T // 2)
            sp.wait_ge(wlo_ready, 3 * (E + 1) - len(POOL_CHUNKS) - 2)
            for i in range(4):
                load_rows(i, i)
            for s in (T - 3, T - 2, T - 1):
                store_shared(s, s % 2)
            with sp.Fori(0, (ET - 3 - 4) // 4) as turn:
                i = sp.snap(turn * 4 + 4)
                for q in range(4):
                    load_rows(i + q, q)
            for i in range(ET - 3, ET):
                load_rows(i, i % 4)

        @block.gpsimd
        def _(pool):
            pool.sem_inc(row_ready, 1)
            pool.sem_inc(xlo_ready, 1)
            pool.memset(tiny[:, :], TINY).then_inc(consts_made, 1)
            pool.memset(pad_row, 0.0).then_inc(tri_zero, 1)
            pool.wait_ge(tri_zero, 1)
            pool.iota(rows[:, T - 1, D + 1:D + 2].bitcast(I32), pattern=[[1, 1]], base=N, channel_multiplier=1
                      ).then_inc(consts_made, 1)
            pool.memset(ident[:, :], 0.0).then_inc(tri_zero, 1)
            pool.wait_ge(tri_zero, 2)
            pool.affine_select(out=ident[:, :], in_=ident[:, :], compare_op=ALU.not_equal, fill=1.0, base=0,
                               pattern=[[-1, P]], channel_multiplier=1).then_inc(consts_made, 1)

            def residual(b, q):
                pool.wait_ge(x_loaded[q], 8 * (b - q) + 16)
                pool.tensor_tensor(x1[:, bass.ds(b * QT, QT), :], x_in[q],
                                   bo[:, :].rearrange("p (o d) -> p o d", o=1).to_broadcast([P, QT, D]), ALU.add
                                   ).then_inc(xb_ready, 1)

            def keep_row(c):
                pool.wait_ge(xf_ready, c + 1)
                pool.tensor_copy(rows[:, bass.ds(c * QT, QT), 0:D], xf).then_inc(row_ready, 1)

            def split_lo(c):
                pool.wait_ge(whi_ready, c + 1)
                pool.tensor_tensor(w_lo[:, c * CH:(c + 1) * CH], stage[c % 2], w_hi[:, c * CH:(c + 1) * CH],
                                   ALU.subtract).then_inc(pool_split, 1)

            def masks(b, q):
                pool.wait_ge(logm_made, b + 1)
                alone(pool, pool_passed)
                pool.tensor_scalar(cm[q], cm[q], 0.0, MASKED, ALU.is_le, ALU.mult).then_inc(pen_ready, 1)
                pool.wait_ge(pen_ready, b + 1)
                pool.tensor_tensor(log_m[:, :, :], log_m[:, :, :], cm[q], ALU.add).then_inc(pen_added, 1)
                pool.wait_ge(seqm_ready, b + 1)
                pool.wait_ge(pen_added, b + 1)
                pool.tensor_tensor(log_m[:, :, :], log_m[:, :, :],
                                   sm_log[:, :].rearrange("p (o k) -> p o k", o=1).to_broadcast([P, QT, S]), ALU.add
                                   ).then_inc(logm_ready, 1)

            pool.memset(ones, 1.0).then_inc(consts_made, 1)
            pool.memset(ones_b[:, :], 1.0).then_inc(consts_made, 1)
            pool.memset(before[:, :], 1.0).then_inc(tri_zero, 1)
            pool.wait_ge(tri_zero, 3)
            pool.affine_select(out=before[:, :], in_=before[:, :], compare_op=ALU.is_gt, fill=0.0, base=0,
                               pattern=[[1, P]], channel_multiplier=-1).then_inc(consts_made, 1)
            masks(0, 0)
            pool.wait_ge(cols_in, 32)
            residual(0, 0)
            residual(1, 1)
            pool.iota(desc[:, :, :], pattern=[[-1, E], [0, T]], base=E, channel_multiplier=0,
                      allow_small_or_imprecise_dtypes=True).then_inc(consts_made, 1)
            pool.iota(tile_no[:, :, :], pattern=[[1, ET], [0, E]], base=0, channel_multiplier=0,
                      allow_small_or_imprecise_dtypes=True).then_inc(consts_made, 1)
            residual(2, 0)
            masks(1, 1)
            with pool.Fori(0, (B - 2 - 2) // 2) as turn:
                b = pool.snap(turn * 2 + 2)
                residual(b + 1, 1)
                masks(b, 0)
                keep_row(b - 2)
                residual(b + 2, 0)
                masks(b + 1, 1)
                keep_row(b - 1)
            residual(B - 1, 1)
            masks(B - 2, 0)
            keep_row(B - 4)
            masks(B - 1, 1)
            keep_row(B - 3)
            split_lo(5)
            keep_row(B - 2)
            split_lo(6)
            pool.wait_ge(pads_written, 16 * (B + 1))
            pool.iota(rows[:, :, D + 1:D + 2].bitcast(I32), pattern=[[P, T], [1, 1]], base=0, channel_multiplier=1
                      ).then_inc(consts_made, 1)
            keep_row(B - 1)
            for c in POOL_CHUNKS[2:]:
                split_lo(c)

            pool.wait_ge(consts_made, 9)
            pool.wait_ge(row_ready, B + 1)
            pool.wait_ge(pos_ready, 1)
            for k in range(TOP_K):
                for half in range(2):
                    if k == 0:
                        pool.wait_ge(w_ready, 1)
                    else:
                        pool.wait_ge(rows_sent[half], 16 * T // 2)
                        some = slice(half * T // 2, (half + 1) * T // 2)
                        pool.tensor_scalar(rows[:, some, D], w2[:, some], SH / (SX * SW), None, ALU.mult
                                           ).then_inc(w_ready, 1)
                        pool.wait_ge(w_ready, 2 + half)
                    for t in range(half * T // 2, (half + 1) * T // 2):
                        pool.indirect_dma_start(dispatch, bass.IndirectOffsetOnAxis(pos[k][:, t:t + 1], 0),
                                                rows[:, t, :], None).then_inc(rows_sent[2 * k + half], 16)

            for i in range(2):
                pool.wait_ge(shared_stored[i], 16 * T // 2)

            def add_rows(i, q):
                pool.wait_ge(y_ready, i + T + 1)
                at_least(pool, added, 16 * i)
                alone(pool, pool_passed)
                pool.indirect_dma_start(out, bass.IndirectOffsetOnAxis(tok[:, q:q + 1], 0), y[q], None,
                                        compute_op=ALU.add).then_inc(added, 16)

            add_rows(0, 0)
            with pool.Fori(0, (ET - 2 - 1) // 4) as turn:
                i = pool.snap(turn * 4 + 1)
                for k in range(4):
                    add_rows(i + k, (1 + k) % 4)
            for i in range(ET - 2, ET):
                add_rows(i, i % 4)
            pool.wait_ge(added, 16 * ET)

        @block.scalar
        def _(act):
            act.preload_act_table_set("natural_log_exp_and_others")

            def split_hi(c, q, loaded=None, count=None):
                act.wait_ge(loaded or w_loaded[q], count if loaded else 8 * (c - q) + 16)
                i = act.activation(w_hi[:, bass.ds(c * CH, CH)], stage[q], ACT.Copy, scale=SW)
                if isinstance(c, int) and c in POOL_CHUNKS:
                    i = act.activation(stage[q], stage[q], ACT.Copy, scale=SW)
                i.then_inc(whi_ready, 1)

            def rough_rstd(n, a, z_):
                act.wait_ge(ve_ready, n)
                act.activation(r0[:, a:z_], ve[:, a:z_], ACT.Ln).then_inc(ln_ready, 1)
                act.wait_ge(ln_ready, n)
                act.activation(r0[:, a:z_], r0[:, a:z_], ACT.Exp, scale=-0.5).then_inc(r0_ready, 1)

            def exps(c, q):
                act.wait_ge(max_ready, c + 1)
                for t in range(QT):
                    e = act.activation(p[:, t, :], p[:, t, :], ACT.Exp, bias=nmax[:, t:t + 1],
                                       accum_out=sums[q][:, t:t + 1])
                e.then_inc(p_ready, 1)

            def k_out(b):
                act.wait_ge(k_done, b + 1)
                for m in range(DC):
                    e = act.activation(k_t[:, m, :], two(bank[1][:, :])[:, m, :], ACT.Identity, bias=col[:, m, 2:3])
                e.then_inc(kt_ready, 1)

            def x_out(b):
                act.wait_ge(tx_done, b + 1)
                act.activation(x_t, two(bank[0][:, :]), ACT.Copy).then_inc(xt_ready, 1)

            def p_out(c):
                act.wait_ge(tp_done, c + 1)
                act.activation(p_t, two(bank[3][:, :]), ACT.Copy).then_inc(pt_ready, 1)

            def a_out(c):
                act.wait_ge(a_done, c + 1)
                act.activation(a_t, two(bank[4][:, :]), ACT.Copy).then_inc(at_ready, 1)

            def xf_hi(c):
                act.wait_ge(txf_done, c + 1)
                act.activation(xt[:, bass.ds(c * QT, QT), 0, :, :],
                               bank[6][:, :].rearrange("p (t c q) -> p t c q", t=QT, c=DC), ACT.Copy, scale=SX
                               ).then_inc(xhi_ready, 1)

            def logs(b, q):
                act.wait_ge(cm_loaded[q], 8 * (b - q) + 16)
                at_least(act, s_masked, b)
                act.activation(log_m[:, :, :], cm[q], ACT.Ln, bias=tiny[:, :])
                at_least(act, logm_ready, b)
                act.wait_ge(sm_loaded, 16 * b + 16)
                act.activation(sm_log[:, :], sm[:, :], ACT.Ln, bias=tiny[:, :]).then_inc(logm_made, 1)

            act.wait_ge(consts_made, 3)
            rough_rstd(1, 2, 4)
            act.wait_ge(cols_in, 32)

            def step(b, q):
                reg = not isinstance(b, int)
                logs(b, q)
                if reg or 1 <= b:
                    exps(b - 1, 1 - q)
                k_out(b)
                if reg or 1 <= b:
                    p_out(b - 1)
                x_out(b)
                rough_rstd(b + 2, 0 if reg or b >= 2 else 2, 4 if reg or b + 1 < B else 2)
                if reg or 3 <= b:
                    xf_hi(b - 3)
                for c in () if reg or b > 2 else FIRST_CHUNKS[b]:
                    split_hi(c, c % 2)
                if reg or 1 <= b:
                    a_out(b - 1)

            step(0, 0)
            step(1, 1)
            step(2, 0)
            with act.Fori(0, (B - 1 - 3) // 2) as turn:
                b = act.snap(turn * 2 + 3)
                step(b, 1)
                step(b + 1, 0)
            step(B - 1, (B - 1) % 2)
            split_hi(5, 1)

            def silu(n, q):
                act.wait_ge(g_done, n + 1)
                at_least(act, h_ready, n)
                act.activation(g_act, bank[2 * q][:, :], ACT.Silu, scale=1.0 / (SX * SW)).then_inc(act_ready, 1)

            def h_out(n):
                act.wait_ge(th_done, n + 1)
                at_least(act, d_done, n)
                act.activation(h_hi, bank[4][:, :], ACT.Copy).then_inc(hhi_ready, 1)

            def xe_out(i, q):
                act.wait_ge(tg_done, i + 1)
                act.activation(xe_hi[q], bank[6][:, 0:D].rearrange("p (c t) -> p c t", c=DC), ACT.Copy, scale=SX
                               ).then_inc(ghi_ready, 1)

            def y_out(n, r):
                act.wait_ge(d_done, n + 1)
                at_least(act, added, 16 * (n - T - 3))
                act.activation(y[r], bank[5][:, 0:D], ACT.Copy, scale=1.0 / (SH * SW)
                               ).then_inc(y_ready, 1)

            xf_hi(B - 3)
            exps(B - 1, (B - 1) % 2)
            p_out(B - 1)
            rough_rstd(B + 2, 0, 2)
            act.preload_act_table(ACT.Silu)
            silu(0, 0)
            a_out(B - 1)
            xf_hi(B - 2)
            split_hi(6, 0)
            split_hi(7, 1)
            h_out(0)
            silu(1, 1)
            act.preload_act_table_set("natural_log_exp_and_others")
            rough_rstd(B + 3, 0, 2)
            xf_hi(B - 1)
            h_out(1)
            act.wait_ge(ve3_ready, 1)
            act.activation(r03, ve3, ACT.Ln).then_inc(ln_ready, 1)
            act.wait_ge(ln_ready, B + 4)
            act.activation(r03, r03, ACT.Exp, scale=-0.5).then_inc(r03_ready, 1)
            act.preload_act_table(ACT.Silu)
            late_pool_chunks = {2: 8, 3: 9, 5: 10}
            for s in range(2, ROUTED):
                if s > 2:
                    h_out(s - 1)
                silu(s, s % 2)
                if s in late_pool_chunks:
                    split_hi(late_pool_chunks[s], late_pool_chunks[s] % 2)
                if s == ROUTED - 3:
                    act.preload_act_table_set("natural_log_exp_and_others")
                    act.wait_ge(d_ready, 1)
                    act.activation(expo, tmp, ACT.Exp).then_inc(expo_ready, 1)
                    act.preload_act_table(ACT.Silu)

            with act.Fori(0, (T - 1 - ROUTED) // 2) as turn:
                t = act.snap(turn)
                for k in range(2):
                    h_out(2 * t + ROUTED + k - 1)
                    silu(2 * t + ROUTED + k, (ROUTED + k) % 2)
                    for m in (2 * k, 2 * k + 1):
                        split_hi(C0 + 4 * t + m, stages[m], late_loaded[m], 16 * t + 16)
            h_out(T - 2)
            silu(T - 1, 1)
            xe_out(0, 0)

            def expert(i, k, more=True, y_too=True):
                h_out(i + T - 1)
                if more:
                    xe_out(i + 1, (k + 1) % 2)
                silu(i + T, k % 2)
                if y_too:
                    y_out(i + T - 1, (k + 3) % 4)

            expert(0, 0, y_too=False)
            act.wait_ge(shared_stored[0], 16 * T // 2)
            act.wait_ge(shared_stored[1], 16 * T // 2)
            for i in range(1, 5):
                expert(i, i % 4)
            with act.Fori(0, (ET - 2 - 5) // 4) as turn:
                i = act.snap(turn * 4 + 5)
                for k in range(4):
                    expert(i + k, (1 + k) % 4)
            expert(ET - 2, (ET - 2) % 4)
            expert(ET - 1, (ET - 1) % 4, more=False)
            h_out(ET + T - 1)
            y_out(ET + T - 1, (ET - 1) % 4)

        @block.vector
        def _(dve):
            def split_lo(c, q):
                dve.wait_ge(whi_ready, c + 1)
                dve.scalar_tensor_tensor(w_lo[:, bass.ds(c * CH, CH)], stage[q], SW,
                                         w_hi[:, bass.ds(c * CH, CH)], ALU.mult, ALU.subtract
                                         ).then_inc(wlo_ready, 1)

            def seq_penalty(b):
                dve.wait_ge(logm_made, b + 1)
                dve.tensor_scalar(sm[:, :], sm[:, :], 0.0, MASKED, ALU.is_le, ALU.mult).then_inc(smp_ready, 1)

            def seq_penalty_added(b):
                dve.wait_ge(smp_ready, b + 1)
                dve.tensor_tensor(sm_log[:, :], sm_log[:, :], sm[:, :], ALU.add).then_inc(seqm_ready, 1)

            def add_mask(c):
                dve.wait_ge(s_done, c + 1)
                dve.wait_ge(logm_ready, c + 1)
                at_least(dve, tp_done, c)
                dve.tensor_tensor(p, two(bank[2][:, :]), log_m[:, :, :], ALU.add).then_inc(s_masked, 1)

            def max_of(c):
                dve.wait_ge(s_masked, c + 1)
                dve.tensor_reduce(nmax[:, :], p, AX.X, ALU.max, negate=True).then_inc(max_ready, 1)

            def nothing():
                pass

            def invert_sums(c, q):
                dve.wait_ge(p_ready, c + 1)
                dve.reciprocal(rinv[:, :], sums[q][:, :]).then_inc(rinv_ready, 1)

            def norms(n, c, b, q, before_means=nothing, before_roots=nothing,
                      before_xf=nothing):
                a, z_ = (0 if c is not None else 2), (4 if b is not None else 2)
                if c is not None:
                    dve.wait_ge(rinv_ready, c + 1)
                    dve.wait_ge(o_done, c + 1)
                    dve.wait_ge(xb_ready, c + 1)
                    for t in range(QT):
                        i = dve.scalar_tensor_tensor(x1[:, bass.ds(c * QT + t, 1), :].rearrange("p o d -> p (o d)"),
                                                     two(bank[5][:, :])[:, t, :], rinv[:, t:t + 1],
                                                     x1[:, bass.ds(c * QT + t, 1), :].rearrange("p o d -> p (o d)"),
                                                     ALU.mult, ALU.add)
                    i.then_inc(x1_ready, 1)
                if b is not None:
                    dve.wait_ge(x_loaded[q], 8 * (b - q) + 16)
                    alone(dve, dve_passed)
                    for t in range(QT):
                        i = dve.bn_stats(stats[:, 2 + t, :], x_in[q][:, t, :])
                if c is not None:
                    dve.wait_ge(x1_ready, c + 1)
                    alone(dve, dve_passed)
                    for t in range(QT):
                        i = dve.bn_stats(stats[:, t, :], x1[:, bass.ds(c * QT + t, 1), :].rearrange("p o d -> p (o d)"))
                i.then_inc(stats_ready, 1)
                before_means()
                dve.wait_ge(stats_ready, n)
                alone(dve, dve_passed)
                for s in range(a, z_):
                    i = dve.bn_aggr(mv[:, s, :], stats[:, s, :])
                i.then_inc(mv_ready, 1)
                dve.wait_ge(mv_ready, n)
                v = ve[:, a:z_]
                dve.tensor_scalar(v, mv[:, a:z_, 1], LN_EPS, None, ALU.add).then_inc(ve_ready, 1)
                before_roots()
                dve.wait_ge(r0_ready, n)
                r = r0[:, a:z_]
                newton(r, v, r2[:, a:z_], rstd[:, a:z_], nt_ready, 3 * (n - 1))
                if b is not None:
                    at_least(dve, tx_done, b)
                    for t in range(QT):
                        i = dve.tensor_scalar(xln[:, t, :], x_in[q][:, t, :], mv[:, 2 + t, 0:1],
                                              rstd[:, 2 + t:3 + t], ALU.subtract, ALU.mult)
                    i.then_inc(xln_ready, 1)
                before_xf()
                if c is not None:
                    dve.wait_ge(row_ready, c + 1)
                    for t in range(QT):
                        i = dve.tensor_scalar(xf[:, t, :],
                                              x1[:, bass.ds(c * QT + t, 1), :].rearrange("p o d -> p (o d)"),
                                              mv[:, t, 0:1], rstd[:, t:t + 1], ALU.subtract, ALU.mult)
                    i.then_inc(xf_ready, 1)

            def newton(r, v, t2, res, chain, base):
                dve.tensor_tensor(t2, r, r, ALU.mult).then_inc(chain, 1)
                dve.wait_ge(chain, base + 1)
                dve.scalar_tensor_tensor(t2, t2, -0.5, v, ALU.mult, ALU.mult).then_inc(chain, 1)
                dve.wait_ge(chain, base + 2)
                dve.scalar_tensor_tensor(res, t2, 1.5, r, ALU.add, ALU.mult).then_inc(chain, 1)
                dve.wait_ge(chain, base + 3)

            def xf_stats(c):
                dve.wait_ge(xf_ready, c + 1)
                alone(dve, dve_passed)
                for t in range(QT):
                    i = dve.bn_stats(stats3[:, t, :], xf[:, t, :])
                i.then_inc(st3_ready, 1)

            def xf_means(c):
                dve.wait_ge(st3_ready, c + 1)
                alone(dve, dve_passed)
                for t in range(QT):
                    i = dve.bn_aggr(mv_xf[:, t, :], stats3[:, t, :])
                i.then_inc(mvx_ready, 1)

            def keep_means(c):
                dve.wait_ge(mvx_ready, c + 1)
                dve.tensor_copy(mv3[:, bass.ds(c * QT, QT), :], mv_xf[:, :, :]).then_inc(mv3_ready, 1)

            def xf_lo(c):
                dve.wait_ge(xhi_ready, c + 1)
                dve.scalar_tensor_tensor(xt[:, bass.ds(c * QT, QT), 1, :, :],
                                         bank[6][:, :].rearrange("p (t c q) -> p t c q", t=QT, c=DC), SX,
                                         xt[:, bass.ds(c * QT, QT), 0, :, :],
                                         ALU.mult, ALU.subtract).then_inc(xlo_ready, 1)

            norms(1, None, 0, 0)
            dve.wait_ge(cols_in, 32)
            for c in range(DC):
                dve.tensor_scalar(gate_bias[:, c, 0:E], col[:, c, 3:3 + E], col[:, c, 0:1], None, ALU.mult)
                i = dve.tensor_scalar(gate_bias[:, c, E:2 * E], col[:, c, 3:3 + E], col[:, c, 1:2], None, ALU.mult)
            i.then_inc(gates_made, 1)
            dve.wait_ge(gates_made, 1)
            dve.tensor_scalar(gate_hi[:, :, :], gate_bias[:, :, 0:E], SG, None, ALU.mult).then_inc(gates_made, 1)
            dve.wait_ge(gates_made, 2)
            dve.scalar_tensor_tensor(gate_lo[:, :, :], gate_bias[:, :, 0:E], SG, gate_hi[:, :, :],
                                     ALU.mult, ALU.subtract).then_inc(gates_made, 1)

            def step(b, q):
                reg = not isinstance(b, int)
                if reg or 2 <= b:
                    invert_sums(b - 2, q)
                if reg or 1 <= b <= B:
                    add_mask(b - 1)
                if reg or 3 <= b:
                    xf_means(b - 3)
                if reg or 1 <= b <= B:
                    max_of(b - 1)

                def before_means():
                    if reg or b < B:
                        seq_penalty(b)

                def before_roots():
                    if reg or b < B:
                        seq_penalty_added(b)
                    if reg or 3 <= b:
                        keep_means(b - 3)

                def before_xf():
                    if reg or 3 <= b:
                        xf_lo(b - 3)

                norms(b + 2, b - 2 if reg or b >= 2 else None, b + 1 if reg or b + 1 < B else None, 1 - q,
                      before_means, before_roots, before_xf)
                if reg or 2 <= b:
                    xf_stats(b - 2)
                for c in () if reg or b > 2 else FIRST_CHUNKS[b]:
                    split_lo(c, c % 2)

            step(0, 0)
            step(1, 1)
            dve.wait_ge(gb_summed, 1)
            dve.tensor_copy(sg_c[:, :, :], bank[7][:, P:P + 2 * E].rearrange("p (a e) -> p a e", a=2)
                            ).then_inc(gb_copied, 1)
            step(2, 0)
            with dve.Fori(0, (B - 1 - 3) // 2) as turn:
                b = dve.snap(turn * 2 + 3)
                step(b, 1)
                step(b + 1, 0)
            step(B - 1, (B - 1) % 2)
            step(B, B % 2)

            def h_mul(n, q, scalar, row=None):
                dve.wait_ge(u_done, n + 1)
                dve.wait_ge(act_ready, n + 1)
                at_least(dve, th_done, n)
                if row is not None:
                    dve.tensor_copy(tok[:, row:row + 1], xg[row][:, D + 1:D + 2].bitcast(U32))
                dve.scalar_tensor_tensor(h, bank[2 * q + 1][:, :], scalar, g_act, ALU.mult, ALU.mult
                                         ).then_inc(h_ready, 1)

            def h_low(n):
                dve.wait_ge(hhi_ready, n + 1)
                dve.tensor_tensor(h_lo, bank[4][:, :], h_hi, ALU.subtract).then_inc(hlo_ready, 1)

            def xe_low(i, q):
                dve.wait_ge(ghi_ready, i + 1)
                dve.scalar_tensor_tensor(xe_lo[q], bank[6][:, 0:D].rearrange("p (c t) -> p c t", c=DC), SX, xe_hi[q],
                                         ALU.mult, ALU.subtract).then_inc(glo_ready, 1)

            def y_shared(s, q):
                dve.wait_ge(d_done, s + 1)
                at_least(dve, shared_stored[q], 8 * (s - q))
                dve.scalar_tensor_tensor(y[q], bank[5][:, 0:D], 1.0 / (SH * SW),
                                         x1[:, bass.ds(s, 1), :].rearrange("p o d -> p (o d)"), ALU.mult, ALU.add
                                         ).then_inc(y_ready, 1)

            count = [0]

            def then(i):
                i.then_inc(route, 1)
                count[0] += 1
                dve.wait_ge(route, count[0])

            def over_experts(ap):
                return ap.rearrange("p (o t) -> p o t", o=1).to_broadcast([P, E, T])

            def over_tiles(ap):
                return ap.rearrange("p (e o) -> p e o", o=1).to_broadcast([P, E, T])

            def flat(ap):
                return ap.rearrange("p e t -> p (e t)")

            def third_norm():
                dve.wait_ge(mv3_ready, B)
                dve.tensor_scalar(ve3, mv3[:, :, 1], LN_EPS, None, ALU.add).then_inc(ve3_ready, 1)

            def logits():
                dve.wait_ge(ve3_ready, 1)
                dve.wait_ge(r03_ready, 1)
                newton(r03, ve3, r23, rs3, route, count[0])
                count[0] += 3
                dve.scalar_tensor_tensor(nm3, mv3[:, :, 0], -1.0, rs3, ALU.mult, ALU.mult)
                then(dve.tensor_scalar(r23, rs3, 1.0 / (SX * SG), None, ALU.mult))
                dve.wait_ge(lg_done, B)
                dve.tensor_tensor(logit, bank[7][:, 0:P].rearrange("p (t e) -> p e t", e=E), over_experts(r23), ALU.mult)
                then(dve.tensor_tensor(tmp, over_tiles(sg_c[:, 0, :]), over_experts(nm3), ALU.mult))
                then(dve.tensor_tensor(logit, logit, tmp, ALU.add))
                then(dve.tensor_tensor(logit, logit, over_tiles(sg_c[:, 1, :]), ALU.add))
                then(dve.tensor_reduce(m1, by_tile(logit), AX.X, ALU.max))

            def choices():
                dve.tensor_tensor(tmp, logit, over_experts(m1), ALU.subtract).then_inc(d_ready, 1)
                dve.wait_ge(d_ready, 1)
                dve.wait_ge(consts_made, 8)
                then(dve.scalar_tensor_tensor(eq, tmp, 0.0, desc[:, :, :], ALU.is_equal, ALU.mult))
                then(dve.tensor_reduce(mx, by_tile(eq), AX.X, ALU.max))
                then(dve.tensor_tensor(one1, desc[:, :, :], over_experts(mx), ALU.is_equal))
                then(dve.scalar_tensor_tensor(logit, one1, -1e30, tmp, ALU.mult, ALU.add))
                then(dve.tensor_reduce(m2, by_tile(logit), AX.X, ALU.max))
                then(dve.tensor_tensor(eq, logit, over_experts(m2), ALU.is_equal))
                then(dve.tensor_tensor(eq, eq, desc[:, :, :], ALU.mult))
                then(dve.tensor_reduce(mx, by_tile(eq), AX.X, ALU.max))
                then(dve.tensor_tensor(one2, desc[:, :, :], over_experts(mx), ALU.is_equal))
                dve.tensor_tensor(both[:, :, :], one1, one2, ALU.add).then_inc(both_ready, 1)

            def places():
                dve.wait_ge(expo_ready, 1)
                then(dve.memset(zero_first, 1.0))
                dve.wait_ge(cum_done, 1)
                then(dve.tensor_copy(tmp, bank[7][:, 2 * P:3 * P].rearrange("p (e t) -> p e t", e=E)))
                then(dve.memset(zero_first[:, :, 0:1], 0.0))
                then(dve.tensor_tensor_scan(flat(cols_incl), flat(zero_first), flat(tmp), 0.0, ALU.mult, ALU.add))
                then(dve.tensor_tensor(offs, cols_incl, tmp, ALU.subtract))
                then(dve.tensor_scalar(n_int[:, 0, :], cols_incl[:, :, T - 1], float(P - 1), None, ALU.add))
                then(dve.tensor_scalar(n_int[:, 1, :], n_int[:, 0, :], 7, None, ALU.logical_shift_right))
                dve.memset(n_e[:, 2, :], 1.0)
                then(dve.tensor_copy(n_e[:, 0, :], n_int[:, 1, :]))
                then(dve.tensor_tensor_scan(n_e[:, 1, :], n_e[:, 2, :], n_e[:, 0, :], 0.0, ALU.mult, ALU.add))
                then(dve.tensor_tensor(n_e[:, 3, :], n_e[:, 1, :], n_e[:, 0, :], ALU.subtract))
                then(dve.tensor_scalar(n_e[:, 3, :], n_e[:, 3, :], float(P), None, ALU.mult))

            def lag(i):
                i.then_inc(route, 1)
                count[0] += 1
                dve.wait_ge(route, count[0] - 1)

            def positions():
                lag(dve.tensor_tensor(offs, offs, over_tiles(n_e[:, 3, :]), ALU.add))
                lag(dve.tensor_reduce(z, by_tile(expo), AX.X, ALU.add))
                lag(dve.tensor_tensor(offs, offs, bank[7][:, 3 * P:4 * P].rearrange("p (e t) -> p e t", e=E), ALU.add))
                lag(dve.tensor_tensor(eq, expo, one2, ALU.mult))
                lag(dve.tensor_tensor(tmp, offs, one1, ALU.mult))
                lag(dve.tensor_reduce(e2, by_tile(eq), AX.X, ALU.add))
                lag(dve.tensor_tensor(logit, offs, one2, ALU.mult))
                lag(dve.tensor_reduce(posf[:, 0, :], by_tile(tmp), AX.X, ALU.add))
                lag(dve.scalar_tensor_tensor(z, z, EPS, e2, ALU.mult, ALU.add))
                lag(dve.tensor_reduce(posf[:, 1, :], by_tile(logit), AX.X, ALU.add))

            def weights_and_tiles():
                lag(dve.tensor_copy(pos[0][:, :], posf[:, 0, :]))
                lag(dve.tensor_scalar(z, z, 1.0, None, ALU.add))
                lag(dve.tensor_copy(pos[1][:, :], posf[:, 1, :]))
                lag(dve.reciprocal(w1, z))
                lag(dve.tensor_tensor(te_cmp[:, :, :], tile_no[:, :, :],
                                      n_e[0:1, 1, :].rearrange("p (o e) -> p o e", o=1).to_broadcast([1, ET, E]), ALU.is_ge))
                lag(dve.tensor_tensor(w2, w1, e2, ALU.mult))
                lag(dve.tensor_reduce(te_f[:, 0, :], te_cmp[:, :, :], AX.X, ALU.add))
                dve.wait_ge(row_ready, B + 1)
                dve.tensor_scalar(rows[:, :, D], w1, SH / (SX * SW), None, ALU.mult).then_inc(w_ready, 1)
                dve.wait_ge(route, count[0])
                then(dve.tensor_scalar(te_f[:, 1, :], te_f[:, 0, :], float(E - 1), 3.0 * CH, ALU.min, ALU.mult))
                dve.tensor_scalar(te[:, :], te_f[:, 1, :], 3.0 * CH, None, ALU.add).then_inc(pos_ready, 1)

            shared_scale = SH / (SX * SW)

            def shared(s, q, meanwhile):
                h_low(s - 1)
                h_mul(s, q, shared_scale)
                meanwhile()
                y_shared(s - 1, 1 - q)

            def shared_and_split():
                with dve.Fori(0, (T - 1 - ROUTED) // 2) as turn:
                    t = dve.snap(turn)
                    for k in range(2):
                        def split_two():
                            for m in (2 * k, 2 * k + 1):
                                split_lo(C0 + 4 * t + m, stages[m])
                        shared(2 * t + ROUTED + k, (ROUTED + k) % 2, split_two)

            h_mul(0, 0, shared_scale)
            xf_lo(B - 2)
            invert_sums(B - 1, (B - 1) % 2)
            xf_means(B - 2)
            norms(B + 3, B - 1, None, None, lambda: keep_means(B - 2), lambda: h_low(0))
            h_mul(1, 1, shared_scale)
            xf_stats(B - 1)
            xf_means(B - 1)
            keep_means(B - 1)
            third_norm()
            xf_lo(B - 1)
            y_shared(0, 0)
            for s, part in enumerate((logits, choices, places, positions, weights_and_tiles), 2):
                shared(s, s % 2, part)
            shared_and_split()
            h_low(T - 2)
            h_mul(T - 1, 1, shared_scale)
            xe_low(0, 0)
            y_shared(T - 2, 0)

            def expert(i, k, more=True):
                h_low(i + T - 1)
                if more:
                    xe_low(i + 1, (k + 1) % 2)
                at_least(dve, added, 16 * (i - 3))
                h_mul(i + T, k % 2, xg[k][:, D:D + 1], k)

            expert(0, 0)
            y_shared(T - 1, 1)
            for i in range(1, 5):
                expert(i, i % 4)
            with dve.Fori(0, (ET - 2 - 5) // 4) as turn:
                i = dve.snap(turn * 4 + 5)
                for k in range(4):
                    expert(i + k, (1 + k) % 4)
            expert(ET - 2, (ET - 2) % 4)
            expert(ET - 1, (ET - 1) % 4, more=False)
            h_low(ET + T - 1)

        @block.tensor
        def _(pe):
            pe.wait_ge(consts_made, 3)

            def transposes(dst, src):
                for c in range(2):
                    for t in range(2):
                        i = pe.transpose(dst[:, c, t * P:(t + 1) * P], src[:, t, c * P:(c + 1) * P], ident[:, :])
                return i

            def products(dst, lhs, rhs):
                for m in range(2):
                    for c in range(2):
                        i = pe.matmul(dst[:, m, :], lhs[:, c, m * P:(m + 1) * P], rhs[:, c, :],
                                      start=(c == 0), stop=(c == 1))
                return i

            def xf_trans(c):
                pe.wait_ge(xf_ready, c + 1)
                pe.wait_ge(xlo_ready, c + 1)
                for t in range(QT):
                    for m in range(DC):
                        i = pe.transpose(bank[6][:, (t * DC + m) * P:(t * DC + m + 1) * P],
                                         xf[:, t, m * P:(m + 1) * P], ident[:, :])
                i.then_inc(txf_done, 1)

            def gate_products(c):
                pe.wait_ge(xlo_ready, c + 2)
                for t in range(c * QT, (c + 1) * QT):
                    for m in range(DC):
                        for j, (part, g) in enumerate(((0, gate_hi), (0, gate_lo), (1, gate_hi))):
                            i = pe.matmul(bank[7][:, t * E:(t + 1) * E], xt[:, t, part, m, :], g[:, m, :],
                                          start=(m == 0 and j == 0), stop=(m == DC - 1 and j == 2))
                i.then_inc(lg_done, 1)

            def output_projection(c):
                pe.wait_ge(at_ready, c + 1)
                at_least(pe, x1_ready, c)
                products(two(bank[5][:, :]), a_t, wo).then_inc(o_done, 1)

            def keys(b, q):
                pe.wait_ge(dk_loaded[q], 8 * (b - q) + 16)
                at_least(pe, kt_ready, b)
                products(two(bank[1][:, :]), wk, c_dk[q]).then_inc(k_done, 1)

            def p_trans(c):
                pe.wait_ge(p_ready, c + 1)
                at_least(pe, pt_ready, c)
                transposes(two(bank[3][:, :]), p).then_inc(tp_done, 1)

            def x_trans(b):
                pe.wait_ge(xln_ready, b + 1)
                at_least(pe, xt_ready, b)
                transposes(two(bank[0][:, :]), xln).then_inc(tx_done, 1)

            def attend(c, q):
                pe.wait_ge(pt_ready, c + 1)
                pe.wait_ge(kd_loaded[q], 8 * (c - q) + 16)
                at_least(pe, at_ready, c)
                products(two(bank[4][:, :]), c_kd[q], p_t).then_inc(a_done, 1)

            def scores(b):
                pe.wait_ge(xt_ready, b + 1)
                pe.wait_ge(kt_ready, b + 1)
                at_least(pe, s_masked, b)
                products(two(bank[2][:, :]), x_t, k_t).then_inc(s_done, 1)

            def step(b, q):
                reg = not isinstance(b, int)
                if reg or 2 <= b:
                    output_projection(b - 2)
                keys(b, q)
                if reg or 1 <= b:
                    p_trans(b - 1)
                x_trans(b)
                if reg or 3 <= b:
                    xf_trans(b - 3)
                if reg or 1 <= b:
                    attend(b - 1, 1 - q)
                scores(b)

            pe.wait_ge(wk_in, 16)
            step(0, 0)
            pe.wait_ge(consts_made, 4)
            pe.wait_ge(gates_made, 3)
            for c in range(DC):
                i = pe.matmul(bank[7][:, P:P + 2 * E], ones, gate_bias[:, c, :], start=(c == 0), stop=(c == DC - 1))
            i.then_inc(gb_summed, 1)
            step(1, 1)
            pe.wait_ge(wo_in, 16)
            step(2, 0)
            pe.wait_ge(gb_copied, 1)
            with pe.Fori(0, (B - 1 - 3) // 2) as turn:
                b = pe.snap(turn * 2 + 3)
                step(b, 1)
                step(b + 1, 0)
            step(B - 1, (B - 1) % 2)

            def three(dst, pairs, last):
                n = len(pairs)
                for j, (a_hi, a_lo, w) in enumerate(pairs):
                    for m, (a, part) in enumerate(((a_hi, 0), (a_hi, 1), (a_lo, 0))):
                        i = pe.matmul(dst, a, w[:, part, :], start=(j == 0 and m == 0), stop=(j == n - 1 and m == 2))
                i.then_inc(last, 1)

            def gate_up(n, q, xh, xl, w, between):
                at_least(pe, act_ready, n - 1)
                three(bank[2 * q][:, :], [(xh(c), xl(c), w[:, :, c * I:(c + 1) * I]) for c in range(DC)], g_done)
                between()
                at_least(pe, h_ready, n - 1)
                three(bank[2 * q + 1][:, :],
                      [(xh(c), xl(c), w[:, :, CH + c * I:CH + (c + 1) * I]) for c in range(DC)], u_done)

            def h_trans(n):
                pe.wait_ge(h_ready, n + 1)
                at_least(pe, hlo_ready, n)
                for j in range(IC):
                    i = pe.transpose(bank[4][:, j * P:(j + 1) * P], h[:, j * P:(j + 1) * P], ident[:, :])
                i.then_inc(th_done, 1)

            def rows_trans(i_, k):
                pe.wait_ge(xg_loaded[k], 4 * (i_ - k) + 16)
                at_least(pe, glo_ready, i_)
                for c in range(DC):
                    i = pe.transpose(bank[6][:, c * P:(c + 1) * P], xg[k][:, c * P:(c + 1) * P], ident[:, :])
                i.then_inc(tg_done, 1)

            def down(n, w):
                pe.wait_ge(hlo_ready, n + 1)
                at_least(pe, y_ready, n)
                three(bank[5][:, 0:D],
                      [(h_hi[:, j * P:(j + 1) * P], h_lo[:, j * P:(j + 1) * P],
                        w[:, :, 2 * CH + j * D:2 * CH + (j + 1) * D])
                       for j in range(IC)], d_done)

            w_shared = w_parts[:, :, 0:3 * CH]

            def shared(s, q, between):
                tokens = xt[:, bass.ds(s, 1)].rearrange("p o m c q -> p (o m) c q")
                gate_up(s, q, lambda c: tokens[:, 0, c, :], lambda c: tokens[:, 1, c, :], w_shared, between)

            def count_rows():
                pe.wait_ge(both_ready, 1)
                pe.wait_ge(consts_made, 6)
                flat = both[:, :, :].rearrange("p e t -> p (e t)")
                pe.matmul(bank[7][:, 2 * P:3 * P], ones_b[:, :], flat, start=True, stop=True)
                pe.matmul(bank[7][:, 3 * P:4 * P], before[:, :], flat, start=True, stop=True).then_inc(cum_done, 1)

            def shared_and_down(s, q):
                shared(s, q, lambda: h_trans(s - 1))
                down(s - 1, w_shared)

            xf_trans(B - 3)
            output_projection(B - 2)
            for c in range(B - 3):
                gate_products(c)
            p_trans(B - 1)
            pe.wait_ge(wlo_ready, 3)
            shared(0, 0, lambda: None)
            attend(B - 1, (B - 1) % 2)
            xf_trans(B - 2)
            gate_products(B - 3)
            output_projection(B - 1)
            gate_products(B - 2)
            shared(1, 1, lambda: h_trans(0))
            pe.wait_ge(x1_ready, B)
            down(0, w_shared)

            def last_tokens():
                xf_trans(B - 1)
                h_trans(1)

            shared(2, 0, last_tokens)
            gate_products(B - 1)
            down(1, w_shared)
            shared_and_down(3, 1)
            shared(4, 0, lambda: h_trans(3))
            count_rows()
            down(3, w_shared)
            for s in range(5, ROUTED):
                shared_and_down(s, s % 2)
            with pe.Fori(0, (T - 1 - ROUTED) // 2) as turn:
                s = pe.snap(turn * 2 + ROUTED)
                for k in range(2):
                    shared_and_down(s + k, (ROUTED + k) % 2)

            shared(T - 1, 1, lambda: h_trans(T - 2))
            rows_trans(0, 0)
            down(T - 2, w_shared)

            pe.wait_ge(pos_ready, 1)
            pe.wait_ge(pool_split, len(POOL_CHUNKS))
            pe.wait_ge(wlo_ready, 3 * (E + 1) - len(POOL_CHUNKS))

            def weights(i):
                off = pe.value_load(te[0:1, bass.ds(i, 1)], min_val=3 * CH, max_val=3 * E * CH)
                return w_parts[:, :, bass.ds(off, 3 * CH)]

            def expert_gate_up(i, k, w):
                pe.wait_ge(glo_ready, i + 1)

                def between():
                    h_trans(i + T - 1)
                    if not isinstance(i, int) or i + 1 < ET:
                        rows_trans(i + 1, (k + 1) % 4)
                gate_up(i + T, k % 2, lambda c: xe_hi[k % 2][:, c, :], lambda c: xe_lo[k % 2][:, c, :], w, between)

            def pairs(j, first, count, w_down, w_up):
                w_mid = None
                for k in range(count):
                    down(j + k + T - 1, w_down)
                    expert_gate_up(j + k + 1, (first + k + 1) % 4, w_up)
                    if k + 1 < count:
                        w_down = weights(j + k) if k == 0 else w_mid
                        w_mid, w_up = w_up, weights(j + k + 2)
                return w_up

            expert_gate_up(0, 0, weights(0))
            pairs(0, 0, 1, w_shared, weights(1))
            with pe.Fori(0, (ET - 3) // 4) as turn:
                j = pe.snap(turn * 4 + 1)
                pairs(j, 1, 4, weights(j - 1), weights(j + 1))
            w_last = pairs(ET - 2, (ET - 2) % 4, 1, weights(ET - 3), weights(ET - 1))
            down(ET + T - 2, weights(ET - 2))
            h_trans(ET + T - 1)
            down(ET + T - 1, w_last)


def kernel(**inputs):
    import numpy as _np
    import concourse.bacc as _bacc
    from concourse import mybir as _mybir
    from concourse.bass_utils import run_bass_kernel_spmd as _run

    f = {k: _np.ascontiguousarray(v) for k, v in inputs.items()}
    pre = "L0_ffn_"

    def packed(w, c):
        w = w.reshape(-1, c, P, w.shape[-1])
        return w.transpose(0, 2, 1, 3).reshape(w.shape[0], P, -1)

    gate, up, down = (_np.concatenate([f[pre + "s" + n][None], f[pre + n]]) for n in ("Wg", "Wu", "Wd"))
    experts = _np.stack([packed(gate, DC), packed(up, DC), packed(down, IC)], axis=1).reshape(3 * (E + 1), P, CH)
    cols = _np.concatenate([f[pre + "ln_scale"][:, None], f[pre + "ln_bias"][:, None],
                            f["L0_xattn_b_k"][:, None], f[pre + "gate_w"].T], axis=1)
    arrays = {
        "x": f["x"].reshape(N, D),
        "ctx_kd": f["ctx_1024"],
        "ctx_dk": f["ctx_1024"].transpose(0, 2, 1),
        "cell_mask": f["mask_BxSxS2_ff1"],
        "seq_mask": f["mask_BxS2_ff1"],
        "wk_t": f["L0_xattn_W_k"].T,
        "wo_t": f["L0_xattn_W_o"].T,
        "b_o": f["L0_xattn_b_o"].reshape(1, D),
        "cols": cols.reshape(DC, P, 3 + E).transpose(1, 0, 2),
        "experts": experts,
    }
    arrays = {f"in_{k}_dram": _np.ascontiguousarray(v) for k, v in arrays.items()}
    nc = _bacc.Bacc("TRN2", target_bir_lowering=False, num_devices=1)
    args = [nc.dram_tensor(k, v.shape, _mybir.dt.from_np(v.dtype), kind="ExternalInput").ap()
            for k, v in arrays.items()]
    dispatch = nc.dram_tensor("dispatch", (B * PADS * P, ROW), _mybir.dt.float32, kind="Internal").ap()
    out = nc.dram_tensor("out_0_dram", (N + P, D), _mybir.dt.float32, kind="ExternalOutput").ap()
    xattn_moe_kernel(nc, *args, dispatch, out)
    r = _run(nc, [arrays], core_ids=[0])
    return r.results[0]["out_0_dram"][:N].reshape(B, S, D)
```
